# Optimizing a Trainium2 kernel written in Bass

```python
import numpy as np
import jax
import jax.numpy as jnp

def _softmax(x, axis=-1):
    return jax.nn.softmax(x, axis=axis)

def _gelu(x):
    return jax.nn.gelu(x, approximate=True)

def _silu(x):
    return jax.nn.silu(x)

def _sigmoid(x):
    return jax.nn.sigmoid(x)

def _layernorm(x, axis=-1, eps=1e-05):
    m = jnp.mean(x, axis=axis, keepdims=True)
    v = jnp.var(x, axis=axis, keepdims=True)
    return (x - m) / jnp.sqrt(v + eps)

def _scatter_add(tgt, idx, src, axis=0):
    return tgt.at[idx].add(src)

def _segment_sum(src, seg, n):
    return jax.ops.segment_sum(src, seg, n)
kernel_name = 'mk_flamingo_gated_d1_seqx_r2_88a314'

def setup_inputs(seed: int=0):
    np.random.seed(seed)
    _w = jnp.asarray

    def _rec_inputs():
        import jax
        import jax.numpy as jnp
        _rk = jax.random.key(seed)
        x = 7.22e-05 + 1 * jax.random.normal(jax.random.fold_in(_rk, 1), (4, 2048, 512), jnp.float32)
        _lenS = 2048 - jax.random.randint(jax.random.fold_in(_rk, 7), (4,), 0, max(1, 2048 // 4) + 1, jnp.int32)
        _lenS2 = 128 - jax.random.randint(jax.random.fold_in(_rk, 8), (4,), 0, max(1, 128 // 4) + 1, jnp.int32)
        _ctx_1024P = jax.random.normal(jax.random.fold_in(_rk, 11), (4, 16, 512), jnp.float32)
        _ctx_1024c = jax.random.dirichlet(jax.random.fold_in(_rk, 511), 0.3 * jnp.ones((16,), jnp.float32), (4, 128))
        _ctx_1024t = jnp.einsum('bsk,bkd->bsd', _ctx_1024c, _ctx_1024P)
        _ctx_1024t = _ctx_1024t * jax.lax.rsqrt(jnp.mean(jnp.square(_ctx_1024t)) + 1e-12) * 0.953939
        ctx_1024 = -1.52775e-05 + 0.999936 * (_ctx_1024t + 0.3 * jax.random.normal(jax.random.fold_in(_rk, 611), (4, 128, 512), jnp.float32))
        _g = jax.random.normal(jax.random.fold_in(_rk, 9001), (2, 1), jnp.float32)
        _g = jnp.sign(_g) * jnp.maximum(jnp.abs(_g), 1.0) + (_g == 0) * 1.0
        g_xattn = _g[0]
        g_ffn = _g[1]
        return (x, ctx_1024, g_xattn, g_ffn)
    x, ctx_1024, g_xattn, g_ffn = _rec_inputs()

    def _L0_xattn_setup():
        import jax, jax.numpy as jnp
        import numpy as np
        HIDDEN = 512
        key = jax.random.key(seed)
        ks = jax.random.split(key, 8)
        s = 1.0 / np.sqrt(HIDDEN)
        return {'query': jax.random.normal(ks[0], (8, 512, HIDDEN), dtype=jnp.float32), 'ref': jax.random.normal(ks[1], (8, 2048, HIDDEN), dtype=jnp.float32), 'Wq': jax.random.normal(ks[2], (HIDDEN, HIDDEN), dtype=jnp.float32) * s, 'bq': jax.random.normal(ks[3], (HIDDEN,), dtype=jnp.float32) * s, 'Wk': jax.random.normal(ks[4], (HIDDEN, HIDDEN), dtype=jnp.float32) * s, 'bk': jax.random.normal(ks[5], (HIDDEN,), dtype=jnp.float32) * s, 'Wv': jax.random.normal(ks[6], (HIDDEN, HIDDEN), dtype=jnp.float32) * s, 'bv': jax.random.normal(ks[7], (HIDDEN,), dtype=jnp.float32) * s}
    _L0_xattn_all = _L0_xattn_setup()
    _L0_xattn_in = {k: v for k, v in _L0_xattn_all.items() if k in ('Wq', 'bq', 'Wk', 'bk', 'Wv', 'bv')}
    del _L0_xattn_all

    def _L0_ffn_setup():
        import jax, jax.numpy as jnp
        import numpy as np
        D_MODEL = 512
        D_FF = 2048
        NUM_EXPERTS = 8
        B, N = (16, 512)
        key = jax.random.key(seed)
        ks = jax.random.split(key, 7)
        s_in = 1.0 / np.sqrt(D_MODEL)
        s_ff = 1.0 / np.sqrt(D_FF)
        return {'x': jax.random.normal(ks[0], (B, N, D_MODEL), dtype=jnp.float32), 'Wr': jax.random.uniform(ks[1], (D_MODEL, NUM_EXPERTS), jnp.float32, -s_in, s_in), 'br': jax.random.uniform(ks[2], (NUM_EXPERTS,), jnp.float32, -s_in, s_in), 'W1': jax.random.uniform(ks[3], (NUM_EXPERTS, D_MODEL, D_FF), jnp.float32, -s_in, s_in), 'b1': jax.random.uniform(ks[4], (NUM_EXPERTS, D_FF), jnp.float32, -s_in, s_in), 'W2': jax.random.uniform(ks[5], (NUM_EXPERTS, D_FF, D_MODEL), jnp.float32, -s_ff, s_ff), 'b2': jax.random.uniform(ks[6], (NUM_EXPERTS, D_MODEL), jnp.float32, -s_ff, s_ff)}
    _L0_ffn_all = _L0_ffn_setup()
    _L0_ffn_in = {k: v for k, v in _L0_ffn_all.items() if k in ('Wr', 'br', 'W1', 'b1', 'W2', 'b2')}
    del _L0_ffn_all
    return {'x': x, 'ctx_1024': ctx_1024, 'g_xattn': g_xattn, 'g_ffn': g_ffn, 'L0_xattn_Wq': _L0_xattn_in['Wq'], 'L0_xattn_bq': _L0_xattn_in['bq'], 'L0_xattn_Wk': _L0_xattn_in['Wk'], 'L0_xattn_bk': _L0_xattn_in['bk'], 'L0_xattn_Wv': _L0_xattn_in['Wv'], 'L0_xattn_bv': _L0_xattn_in['bv'], 'L0_ffn_Wr': _L0_ffn_in['Wr'], 'L0_ffn_br': _L0_ffn_in['br'], 'L0_ffn_W1': _L0_ffn_in['W1'], 'L0_ffn_b1': _L0_ffn_in['b1'], 'L0_ffn_W2': _L0_ffn_in['W2'], 'L0_ffn_b2': _L0_ffn_in['b2']}

def reference(x, ctx_1024, g_xattn, g_ffn, L0_xattn_Wq, L0_xattn_bq, L0_xattn_Wk, L0_xattn_bk, L0_xattn_Wv, L0_xattn_bv, L0_ffn_Wr, L0_ffn_br, L0_ffn_W1, L0_ffn_b1, L0_ffn_W2, L0_ffn_b2):
    import jax
    import jax.numpy as jnp

    def _L0_xattn_ref(query, ref, Wq, bq, Wk, bk, Wv, bv):
        import jax, jax.numpy as jnp
        import numpy as np
        HIDDEN = 512
        norm_fact = 1.0 / np.sqrt(HIDDEN).astype(np.float32)
        Q = query @ Wq + bq
        K = ref @ Wk + bk
        V = ref @ Wv + bv
        scores = jnp.einsum('bqh,bkh->bqk', Q, K)
        attn = jax.nn.softmax(scores, axis=-1) * norm_fact
        return jnp.einsum('bqk,bkh->bqh', attn, V)

    def _L0_ffn_ref(x, Wr, br, W1, b1, W2, b2):
        import jax, jax.numpy as jnp
        import numpy as np
        D_MODEL = 512
        D_FF = 2048
        NUM_EXPERTS = 8
        B, N = (16, 512)
        scores = jnp.einsum('bh,he->be', x.mean(axis=1), Wr) + br
        top1 = jnp.argmax(scores, axis=-1)
        w1 = W1[top1]
        c1 = b1[top1]
        w2 = W2[top1]
        c2 = b2[top1]
        h = jax.nn.relu(jnp.einsum('bnh,bhf->bnf', x, w1) + c1[:, None, :])
        out = jnp.einsum('bnf,bfh->bnh', h, w2) + c2[:, None, :]
        return out
    x = x + jnp.tanh(g_xattn[0]) * _L0_xattn_ref(_layernorm(x, axis=-1), ctx_1024, L0_xattn_Wq, L0_xattn_bq, L0_xattn_Wk, L0_xattn_bk, L0_xattn_Wv, L0_xattn_bv)
    x = x + jnp.tanh(g_ffn[0]) * _L0_ffn_ref(_layernorm(x, axis=-1), L0_ffn_Wr, L0_ffn_br, L0_ffn_W1, L0_ffn_b1, L0_ffn_W2, L0_ffn_b2)
    return x

_drawn_inputs = setup_inputs


def setup_inputs(seed=0):
    import zlib

    import numpy as np

    out = dict(_drawn_inputs(seed))
    spreads = {}
    factors = {'L0_xattn_bq': 22.725,
     'L0_xattn_bk': 64.0,
     'L0_xattn_bv': 38.444,
     'L0_ffn_b1': 5.918,
     'L0_ffn_b2': 4.733}
    for name, (base, spread) in spreads.items():
        noise = np.random.default_rng([zlib.crc32(name.encode()), seed]).standard_normal(out[name].shape)
        drawn = base * np.exp(spread * noise) if base else spread * noise
        out[name] = jnp.asarray(drawn.astype(out[name].dtype))
    for name, factor in factors.items():
        out[name] = (out[name] * factor).astype(out[name].dtype)
    return out
```

```python
from contextlib import ExitStack

import concourse.bass as bass
from concourse import mybir

F32 = mybir.dt.float32
F32R = mybir.dt.float32r
U32 = mybir.dt.uint32
ALU = mybir.AluOpType
ACT = mybir.ActivationFunctionType
AX_X = mybir.AxisListType.X

P = 128
BATCH, SEQ, D = 4, 2048, 512
KEYS = 128
HIDDEN = 2048
EXPERTS = 8
KD = D // P
ROWS = 512
TPB = ROWS // P
BLOCKS = BATCH * SEQ // ROWS
BPS = SEQ // ROWS
TILES = BLOCKS * TPB
TPS = SEQ // P
FC = HIDDEN // P
LEAD = BPS + 1
RING = 4
AHEAD = 3
EPS = 1e-5
NORM = float(D) ** -0.5
BIG = 3.0e38
K_NEWTON = 0.5 ** (1.0 / 3.0)
S_NEWTON = 3.0 * K_NEWTON * K_NEWTON


def gated_block(nc, x, ctx_in, g_xattn, g_ffn, wq, bq, wk, bk, wv, bv, wr, br, w1, b1, w2, b2, ident_in, rank_in, out):
    ctx = ExitStack()
    with ctx:
        def sb(name, shape, dt=F32):
            return ctx.enter_context(nc.sbuf_tensor(name, shape, dt))

        def sem(name):
            return ctx.enter_context(nc.semaphore(name))

        x2_dram = nc.dram_tensor("x2_dram", (TILES, P, D), F32, kind="Internal").ap()
        xn2T_dram = nc.dram_tensor("xn2T_dram", (TILES, P, KD, P), F32, kind="Internal").ap()

        w_raw = sb("w_raw", [P, FC, 2 * D + 1])
        w_hi = sb("w_hi", [P, RING, 2 * D], F32R)
        w_lo = sb("w_lo", [P, RING, 2 * D], F32R)
        b1_cur = sb("b1_cur", [P, FC])
        b2_cur = sb("b2_cur", [P, D])
        xn2T_raw = sb("xn2T_raw", [P, TPB, KD, P])
        xn2T_hi = sb("xn2T_hi", [P, 2, KD, ROWS], F32R)
        xn2T_lo = sb("xn2T_lo", [P, 2, KD, ROWS], F32R)
        x2_blk = sb("x2_blk", [P, TPB, D])
        h_full = sb("h_full", [P, 2, ROWS])
        h_hi = sb("h_hi", [P, 2, ROWS], F32R)
        h_lo = sb("h_lo", [P, 2, ROWS], F32R)
        m_all = sb("m_all", [P, KD, BATCH * KEYS])
        v_all = sb("v_all", [P, BATCH, D])
        cb_all = sb("cb_all", [P, BATCH * KEYS])
        ident = sb("ident", [P, P])
        wr_sb = sb("wr_sb", [P, KD, EXPERTS])
        br_sb = sb("br_sb", [1, EXPERTS])
        gates = sb("gates", [P, 2])
        gate_x = sb("gate_x", [P, 1])
        gate_f = sb("gate_f", [P, 1])
        eps_c = sb("eps_c", [P, 1])
        lnk_c = sb("lnk_c", [P, 1])
        bk_sb = sb("bk_sb", [P, KD])
        bq_sb = sb("bq_sb", [P, KD])
        x_ring = sb("x_ring", [P, 4, D])
        xn = sb("xn", [P, D])
        xnT = sb("xnT", [P, KD, P])
        neg_s = sb("neg_s", [P, KEYS])
        neg_max = sb("neg_max", [P, 1])
        probs = sb("probs", [P, KEYS])
        p_sum = sb("p_sum", [P, 1])
        p_inv = sb("p_inv", [P, 1])
        coef = sb("coef", [P, 1])
        pT = sb("pT", [P, P])
        xn2 = sb("xn2", [P, D])
        xn2T_st = sb("xn2T_st", [P, 2, KD, P])
        tok_sums = sb("tok_sums", [P, KD, TPS])
        stats = [sb(f"stats{n}", [P, 6]) for n in (1, 2)]
        mean_var = [sb(f"mean_var{n}", [P, 2]) for n in (1, 2)]
        ln_v = [sb(f"ln_v{n}", [P, 1]) for n in (1, 2)]
        y_k = [sb(f"y_k{n}", [P, 1]) for n in (1, 2)]
        y_sq = [sb(f"y_sq{n}", [P, 1]) for n in (1, 2)]
        newton = [sb(f"newton{n}", [P, 1]) for n in (1, 2)]
        neg_rstd = [sb(f"neg_rstd{n}", [P, 1]) for n in (1, 2)]
        xsum = sb("xsum", [P, KD])
        logits = sb("logits", [1, EXPERTS])
        rank_down = sb("rank_sb", [1, EXPERTS])
        top = sb("top", [1, 1])
        reach = sb("reach", [1, EXPERTS])
        best_rank = sb("best_rank", [1, 1])
        expert = sb("expert", [1, BLOCKS + 1], U32)

        def in_w(at, n):
            per = (2 * D + 1) * FC
            flat = w_raw[:].rearrange("p f n -> p (f n)")
            assert (at + 1) * KD * D <= per
            return flat[:, at * KD * D:at * KD * D + KD * n].rearrange("p (k n) -> p k n", k=KD)

        ctx_sb, wk_sb, wq_sb, wv_sb = (in_w(i, D) for i in range(4))
        ctxT, wqT, kT = (in_w(i, D) for i in range(4, 7))
        bqb = in_w(7, P)
        bv_sb = x2_blk[:, 0, :]

        bank = [ctx.enter_context(nc.psum_tensor(f"bank{i}", [P, 512], F32)) for i in range(8)]
        out_bank = bank[0:4]
        h_bank = bank[4:6]
        bank_a, bank_b = bank[6], bank[7]

        ctx_in_sem, wk_in, wq_in, wv_in, small_in = (sem(n) for n in ("ctx_in", "wk_in", "wq_in", "wv_in", "small_in"))
        setup_mm, setup_act, setup_dve, consts_done = (sem(n) for n in ("setup_mm", "setup_act", "setup_dve", "consts_done"))
        gates_done = sem("gates_done")
        x_loaded = [sem(f"x_loaded{i}") for i in range(4)]
        x2_stored = [sem(f"x2_stored{i}") for i in range(4)]
        xn2T_stored = [sem(f"xn2T_stored{i}") for i in range(2)]
        st_done = [sem(f"st_done{n}") for n in (1, 2)]
        mv_done = [sem(f"mv_done{n}") for n in (1, 2)]
        lnv_done = [sem(f"lnv_done{n}") for n in (1, 2)]
        yk_done = [sem(f"yk_done{n}") for n in (1, 2)]
        ysq_done = [sem(f"ysq_done{n}") for n in (1, 2)]
        newton_done = [sem(f"newton_done{n}") for n in (1, 2)]
        rstd_done = [sem(f"rstd_done{n}") for n in (1, 2)]
        xn_done, xnT_mm, xnT_done = sem("xn_done"), sem("xnT_mm"), sem("xnT_done")
        s_mm, negs_done, s_read, p_done = (sem(n) for n in ("s_mm", "negs_done", "s_read", "p_done"))
        pT_mm, pT_done = sem("pT_mm"), sem("pT_done")
        pinv_done, coef_done, o_mm, x2_done = (sem(n) for n in ("pinv_done", "coef_done", "o_mm", "x2_done"))
        xn2_done, xn2T_mm, xn2T_done, sum_done = (sem(n) for n in ("xn2_done", "xn2T_mm", "xn2T_done", "sum_done"))
        xsum_done, router_mm, logits_done, top_done, reach_done, rank_done, expert_done = (
            sem(n) for n in ("xsum_done", "router_mm", "logits_done", "top_done", "reach_done", "rank_done", "expert_done"))
        w_loaded = [sem(f"w_loaded{f}") for f in range(FC)]
        b2_loaded = sem("b2_loaded")
        w_hi_done, w_lo_done, w_slot_free = sem("w_hi_done"), sem("w_lo_done"), sem("w_slot_free")
        xn2T_loaded, x2_loaded, out_stored = sem("xn2T_loaded"), sem("x2_loaded"), sem("out_stored")
        xhi_done, xlo_done = sem("xhi_done"), sem("xlo_done")
        h_mm, h_bank_free, h_hi_done, h_lo_done = (sem(n) for n in ("h_mm", "h_bank_free", "h_hi_done", "h_lo_done"))
        b2_added, out_mm, out_bank_free = sem("b2_added"), sem("out_mm"), sem("out_bank_free")

        def rows_of(w):
            return w.rearrange("(k p) n -> p k n", p=P)

        def loop(eng, lo, hi):
            return nc.Fori(lo, hi, engines=[eng.engine], hint_back_edge=True)

        def held(eng, v):
            return v if type(v) is int else eng.snap(eng.to_reg(v) if eng.engine == mybir.EngineType.SP else v)

        def wait(eng, s, v):
            if type(v) is not int or v > 0:
                eng.wait_ge(s, v)

        def sequence_of(eng, blk):
            return blk // BPS if type(blk) is int else nc.s_assert_within(eng.snap(blk >> 2), 0, BATCH - 1, skip_runtime_bounds_check_because="the loop ends at a fixed block")

        def parity(eng, blk):
            return at(blk % 2 if type(blk) is int else nc.s_assert_within(eng.snap(blk & 1), 0, 1, skip_runtime_bounds_check_because="the loop ends at a fixed block"), 1)

        def at(start, size):
            return slice(start, start + size) if type(start) is int else bass.ds(start, size)

        block = ctx.enter_context(nc.Block())

        @block.sync
        def _(sp):
            x2_blocks = x2_dram.rearrange("(s t) p n -> s p t n", t=TPB)
            xn2T_blocks = xn2T_dram.rearrange("(s t) p k n -> s p t k n", t=TPB)

            def load_x(m, q):
                sp.dma_start(x_ring[:, q, :], x[m, q]).then_inc(x_loaded[q], 16)

            def store_x2(m, q):
                n = held(sp, 4 * m + q + 1)
                wait(sp, x2_done, n)
                sp.dma_start(x2_dram[n - 1], x_ring[:, q, :]).then_inc(x2_stored[q], 16)

            def store_xn2T(m, q):
                n = held(sp, 4 * m + q + 1)
                wait(sp, xn2T_done, n)
                sp.dma_start(xn2T_dram[n - 1], xn2T_st[:, q % 2]).then_inc(xn2T_stored[q % 2], 16)

            def attention_slot(m, q, last=False):
                first = type(m) is int and m == 0
                if q > 0:
                    store_x2(m, q - 1)
                elif not first:
                    store_x2(m - 1, 3)
                if q > 1:
                    store_xn2T(m, q - 2)
                elif not first:
                    store_xn2T(m - 1, q + 2)
                if first and q == 0:
                    load_x(m, 3)
                elif q == 0 or not last:
                    stored, normed = held(sp, 16 * (m + 1) if q else 16 * m), held(sp, 4 * m + q)
                    wait(sp, x2_stored[(q + 3) % 4], stored)
                    wait(sp, xn2_done, normed)
                    if q == 0:
                        load_x(m, 3)
                    else:
                        load_x(m + 1, q - 1)

            def load_chunks(e, f0, f1, used):
                for f in range(f0, f1):
                    if used is not None:
                        wait(sp, w_lo_done, held(sp, used + f + 1))
                    cols = slice(f * P, (f + 1) * P)
                    sp.dma_start(w_raw[:, f, 0:D].rearrange("p (k n) -> p k n", k=KD),
                                 w1[bass.ds(e, 1), :, cols].rearrange("e (k p) n -> p (e k) n", p=P)).then_inc(w_loaded[f], 16)
                    sp.dma_start(w_raw[:, f, D:2 * D], w2[bass.ds(e, 1), cols, :].rearrange("e p n -> p (e n)")).then_inc(w_loaded[f], 16)
                    with nc.allow_non_contiguous_dma(reason="one bias per partition"):
                        sp.dma_start(w_raw[:, f, 2 * D:2 * D + 1],
                                     b1[bass.ds(e, 1), cols].rearrange("e p -> p e")).then_inc(w_loaded[f], 16)

            def load_b2(e, used):
                if used is not None:
                    wait(sp, b2_added, held(sp, used))
                sp.dma_start(b2_cur[:], b2[bass.ds(e, 1), :].rearrange("e n -> (e n)").partition_broadcast(P)).then_inc(b2_loaded, 16)

            def chosen(m):
                wait(sp, expert_done, held(sp, m))
                return sp.value_load(expert[0:1, m:m + 1], min_val=0, max_val=EXPERTS - 1)

            def load_xn2T(s):
                stored, split = held(sp, 32 * s + 32), held(sp, KD * s)
                for par in range(2):
                    wait(sp, xn2T_stored[par], stored)
                wait(sp, xhi_done, split)
                wait(sp, xlo_done, split)
                sp.dma_start(xn2T_raw[:], xn2T_blocks[s]).then_inc(xn2T_loaded, 16)

            def store_out(s):
                wait(sp, out_bank_free, held(sp, 4 * s + 8))
                sp.dma_start(out[s], x2_blk[:]).then_inc(out_stored, 16)

            def load_x2(s):
                stored, free = held(sp, 16 * s + 16), held(sp, 16 * s)
                for q in range(TPB):
                    wait(sp, x2_stored[q], stored)
                wait(sp, out_stored, free)
                sp.dma_start(x2_blk[:], x2_blocks[s]).then_inc(x2_loaded, 16)

            def ffn_block(s, att=True, last_att=False, switch=False):
                if att:
                    attention_slot(s + LEAD, 0, last_att)
                if not (type(s) is int and s == 0):
                    store_out(s - 1)
                if type(s) is not int or s < BLOCKS - 1:
                    load_xn2T(s + 1)
                load_x2(s)
                if switch:
                    e = chosen(s + LEAD)
                    load_chunks(e, 0, 4, FC * s)
                for q in range(1, TPB):
                    if att:
                        attention_slot(s + LEAD, q, last_att)
                    if switch:
                        load_chunks(e, 4 * q, 4 * q + 4, FC * s)
                if switch:
                    load_b2(e, 4 * s + 4)

            sp.dma_start(ident[:], ident_in).then_inc(ctx_in_sem, 16)
            sp.dma_start(ctx_sb, ctx_in.rearrange("b p n -> p b n")).then_inc(ctx_in_sem, 16)
            sp.dma_start(wk_sb, rows_of(wk)).then_inc(wk_in, 16)
            with nc.allow_non_contiguous_dma(reason="small vectors, one value per partition"):
                sp.dma_start(bk_sb[:], bk.rearrange("(k p) -> p k", p=P)).then_inc(small_in, 16)
                sp.dma_start(bq_sb[:], bq.rearrange("(k p) -> p k", p=P)).then_inc(small_in, 16)
            sp.dma_start(bv_sb, bv.partition_broadcast(P)).then_inc(small_in, 16)
            sp.dma_start(gates[:, 0:1], g_xattn.partition_broadcast(P)).then_inc(small_in, 16)
            sp.dma_start(gates[:, 1:2], g_ffn.partition_broadcast(P)).then_inc(small_in, 16)
            sp.dma_start(wr_sb[:], rows_of(wr)).then_inc(small_in, 16)
            sp.dma_start(br_sb[:], br[None, :]).then_inc(small_in, 16)
            sp.dma_start(rank_down[:], rank_in).then_inc(small_in, 16)
            sp.dma_start(wq_sb, rows_of(wq)).then_inc(wq_in, 16)
            sp.dma_start(wv_sb, rows_of(wv)).then_inc(wv_in, 16)
            for q in range(3):
                load_x(0, q)

            for q in range(TPB):
                attention_slot(0, q)
            with loop(sp, 1, LEAD - 1) as m:
                for q in range(TPB):
                    attention_slot(m, q)
            attention_slot(LEAD - 1, 0)
            load_xn2T(0)
            e = chosen(LEAD - 1)
            load_chunks(e, 0, 3, None)
            for q in range(1, TPB):
                attention_slot(LEAD - 1, q)
                load_chunks(e, 4 * q - 1, min(4 * q + 3, FC), None)
            load_chunks(e, 15, 16, None)
            load_b2(e, None)

            ffn_block(0)
            with loop(sp, 1, 3) as s:
                ffn_block(s)
            ffn_block(3, switch=True)
            with loop(sp, 4, 7) as s:
                ffn_block(s)
            ffn_block(7, switch=True)
            with loop(sp, 8, 10) as s:
                ffn_block(s)
            ffn_block(10, last_att=True)
            store_x2(BLOCKS - 1, 3)
            store_xn2T(BLOCKS - 1, 2)
            store_xn2T(BLOCKS - 1, 3)
            ffn_block(11, att=False, switch=True)
            with loop(sp, 12, 15) as s:
                ffn_block(s, att=False)
            ffn_block(15, att=False)
            store_out(15)
            sp.wait_ge(out_stored, 16 * BLOCKS)
            for q in range(4):
                sp.wait_ge(x2_stored[q], 16 * BLOCKS)
            for par in range(2):
                sp.wait_ge(xn2T_stored[par], 32 * BLOCKS)

        @block.tensor
        def _(pe):
            def mm(dst, lhsT, rhs, start, stop):
                return pe.matmul(dst, lhsT, rhs, start=start, stop=stop)

            def transpose_xn(n):
                wait(pe, xn_done, n)
                wait(pe, xn2T_done, held(pe, n - 2))
                for k in range(KD):
                    last = pe.transpose(bank_b[:, k * P:(k + 1) * P], xn[:, k * P:(k + 1) * P], ident[:])
                last.then_inc(xnT_mm, 1)

            def scores(n, b):
                wait(pe, xnT_done, n)
                wait(pe, x2_done, held(pe, n - 1))
                for k in range(KD):
                    last = mm(bank_a[:, 0:KEYS], xnT[:, k, :], m_all[:, k, b], k == 0, k == KD - 1)
                last.then_inc(s_mm, 1)

            def transpose_p(n):
                wait(pe, p_done, n)
                pe.transpose(bank_a[:, 0:P], probs[:], ident[:]).then_inc(pT_mm, 1)

            def transpose_xn2(n):
                wait(pe, xn2_done, n)
                wait(pe, xnT_done, TILES if type(n) is int and n == TILES else held(pe, n + 1))
                for k in range(KD):
                    last = pe.transpose(bank_b[:, k * P:(k + 1) * P], xn2[:, k * P:(k + 1) * P], ident[:])
                last.then_inc(xn2T_mm, 1)

            def attend(n, b):
                wait(pe, pT_done, n)
                mm(bank_a[:], pT[:], v_all[:, at(b, 1), :].rearrange("p o n -> p (o n)"), True, True).then_inc(o_mm, 1)

            def router(m):
                wait(pe, xsum_done, held(pe, m))
                for k in range(KD):
                    last = mm(bank_a[0:1, 0:EXPERTS], xsum[:, k:k + 1], wr_sb[:, k, :], k == 0, k == KD - 1)
                last.then_inc(router_mm, 1)

            def slot_parts(m, q, last_tile=False):
                first = type(m) is int and m == 0 and q == 0
                n = held(pe, 4 * m + q + 1)
                b = sequence_of(pe, m)

                def part0():
                    if q == 1:
                        wait(pe, logits_done, held(pe, m))
                    scores(n, at(b * KEYS, KEYS))

                def part1():
                    transpose_p(n)
                    if not first:
                        transpose_xn2(held(pe, n - 1))

                def part2():
                    attend(n, b)
                    if not last_tile:
                        transpose_xn(held(pe, n + 1))

                def part3():
                    if q == 0 and not (type(m) is int and m == 0):
                        router(m)
                return part0, part1, part2, part3

            def ffn_up(c, f, xs):
                wait(pe, w_lo_done, held(pe, c + 1))
                wait(pe, h_bank_free, held(pe, c + 1))
                dst, slot = h_bank[f % 2][:], f % RING
                for k in range(KD):
                    hi = w_hi[:, slot, k * P:(k + 1) * P]
                    lo = w_lo[:, slot, k * P:(k + 1) * P]
                    mm(dst, hi, xn2T_hi[:, xs, k, :].rearrange("p o n -> p (o n)"), k == 0, False)
                    mm(dst, hi, xn2T_lo[:, xs, k, :].rearrange("p o n -> p (o n)"), False, False)
                    last = mm(dst, lo, xn2T_hi[:, xs, k, :].rearrange("p o n -> p (o n)"), False, k == KD - 1)
                last.then_inc(h_mm, 1)

            def ffn_down(c, f):
                slot = f % RING
                whi, wlo = w_hi[:, slot, D:2 * D], w_lo[:, slot, D:2 * D]
                n = held(pe, c + 1)
                wait(pe, h_hi_done, n)
                for t in range(TPB):
                    if f == 0:
                        wait(pe, out_bank_free, held(pe, 4 * (c // FC) + t + 1 if type(c) is int else (c >> 2) + t + 1))
                    cols = slice(t * P, (t + 1) * P)
                    mm(out_bank[t][:], h_hi[:, f % 2, cols], whi, f == 0, False)
                    mm(out_bank[t][:], h_hi[:, f % 2, cols], wlo, False, False)
                wait(pe, h_lo_done, n)
                for t in range(TPB):
                    last = mm(out_bank[t][:], h_lo[:, f % 2, t * P:(t + 1) * P], whi, False, f == FC - 1)
                    if f == FC - 1 and t < TPB - 1:
                        last.then_inc(out_mm, 1)
                last.then_inc(w_slot_free, 1)

            def ffn_block(s, att=True, last_att=False):
                xs = parity(pe, s)
                wait(pe, xlo_done, held(pe, KD * s + KD))
                for f in range(FC):
                    c = FC * s + f
                    if att and f % 4 == 0:
                        parts = slot_parts(s + LEAD, f // 4, last_att and f == 12)
                    ffn_up(c, f, xs)
                    if f > 0:
                        ffn_down(c - 1, f - 1)
                    if att:
                        parts[f % 4]()
                ffn_down(FC * s + FC - 1, FC - 1)

            pe.wait_ge(ctx_in_sem, 32)
            for k in range(KD):
                for b in range(BATCH):
                    last = pe.transpose(bank[k][:, b * P:(b + 1) * P], ctx_sb[:, b, k * P:(k + 1) * P], ident[:])
                last.then_inc(setup_mm, 1)
            pe.wait_ge(wk_in, 16)
            pe.wait_ge(setup_act, KD)
            for h in range(KD):
                for k in range(KD):
                    last = mm(bank[h][:], wk_sb[:, k, h * P:(h + 1) * P], ctxT[:, k, :], k == 0, k == KD - 1)
                last.then_inc(setup_mm, 1)
            pe.wait_ge(wq_in, 16)
            for h in range(KD):
                for k in range(KD):
                    last = pe.transpose(bank[4 + h][:, k * P:(k + 1) * P], wq_sb[:, k, h * P:(h + 1) * P], ident[:])
                last.then_inc(setup_mm, 1)
            pe.wait_ge(wv_in, 16)
            for b in range(BATCH):
                pe.wait_ge(setup_dve, b + 1)
                for k in range(KD):
                    last = mm(bank[4 + b][:], ctxT[:, k, b * KEYS:(b + 1) * KEYS], wv_sb[:, k, :], k == 0, k == KD - 1)
                last.then_inc(setup_mm, 1)
            pe.wait_ge(setup_act, 2 * KD)
            for d in range(KD):
                for h in range(KD):
                    last = mm(bank[d][:], wqT[:, h, d * P:(d + 1) * P], kT[:, h, :], h == 0, h == KD - 1)
                last.then_inc(setup_mm, 1)
            pe.wait_ge(setup_dve, KD + 1)
            pe.wait_ge(consts_done, 4)
            for h in range(KD):
                last = mm(bank[4][:], bqb[:, h, :], kT[:, h, :], h == 0, h == KD - 1)
            last.then_inc(setup_mm, 1)

            pe.sem_inc(w_slot_free, RING)

            pe.wait_ge(setup_act, 3 * KD)
            pe.wait_ge(setup_dve, 2 * KD + 1)
            transpose_xn(1)
            for q in range(TPB):
                for part in slot_parts(0, q):
                    part()
            with loop(pe, 1, LEAD) as m:
                for q in range(TPB):
                    for part in slot_parts(m, q):
                        part()

            with loop(pe, 0, BLOCKS - LEAD - 1) as s:
                ffn_block(s)
            ffn_block(BLOCKS - LEAD - 1, last_att=True)
            transpose_xn2(TILES)
            router(BLOCKS)
            with loop(pe, BLOCKS - LEAD, BLOCKS) as s:
                ffn_block(s, att=False)

        @block.scalar
        def _(act):
            A = nc.scalar.activation

            def ln_root(n, w):
                wait(act, mv_done[w], n)
                A(ln_v[w][:], mean_var[w][:, 1:2], ACT.Ln, bias=eps_c[:]).then_inc(lnv_done[w], 1)
                wait(act, lnv_done[w], n)
                A(y_k[w][:], ln_v[w][:], ACT.Exp, bias=lnk_c[:], scale=-0.5).then_inc(yk_done[w], 1)
                wait(act, yk_done[w], n)
                A(y_sq[w][:], y_k[w][:], ACT.Square).then_inc(ysq_done[w], 1)

            def exp_scores(n):
                wait(act, s_read, n)
                A(probs[:], neg_s[:], ACT.Exp, bias=neg_max[:], scale=-1.0, accum_out=p_sum[:]).then_inc(p_done, 1)

            def copy_pT(n):
                wait(act, pT_mm, n)
                wait(act, o_mm, held(act, n - 1))
                A(pT[:], bank_a[:, 0:P], ACT.Copy).then_inc(pT_done, 1)

            def copy_xnT(n):
                wait(act, xnT_mm, n)
                wait(act, s_mm, held(act, n - 1))
                A(xnT[:].rearrange("p k n -> p (k n)"), bank_b[:], ACT.Copy, scale=-1.0).then_inc(xnT_done, 1)

            def copy_xn2T(n, q, m):
                wait(act, xn2T_mm, n)
                wait(act, xn2T_stored[q % 2], held(act, 32 * m + 16 * (q // 2)))
                wait(act, sum_done, held(act, n - 2))
                A(xn2T_st[:, q % 2].rearrange("p k n -> p (k n)"), bank_b[:], ACT.Copy, scale=-1.0).then_inc(xn2T_done, 1)

            def slot_parts(m, q, last_tile=False):
                first = type(m) is int and m == 0 and q == 0
                n = held(act, 4 * m + q + 1)

                def part0():
                    exp_scores(n)

                def part1():
                    copy_pT(n)
                    if not last_tile:
                        ln_root(held(act, n + 1), 0)

                def part2():
                    if not first:
                        if q > 0:
                            copy_xn2T(held(act, n - 1), q - 1, m)
                        else:
                            copy_xn2T(held(act, n - 1), 3, m - 1)
                    if not last_tile:
                        copy_xnT(held(act, n + 1))

                def part3():
                    ln_root(n, 1)
                return part0, part1, part2, part3

            def split_hi(c, f, b):
                wait(act, w_loaded[f], held(act, 48 * b + 48))
                wait(act, w_slot_free, held(act, c + 1))
                A(w_hi[:, f % RING, :], w_raw[:, f, 0:2 * D], ACT.Copy).then_inc(w_hi_done, 1)

            def split_xn2T(s, k):
                if k == 0:
                    wait(act, xn2T_loaded, held(act, 16 * s + 16))
                par = parity(act, s)
                A(xn2T_hi[:, par, k, :].rearrange("p o (t n) -> p (o t) n", n=P), xn2T_raw[:, :, k, :], ACT.Copy).then_inc(xhi_done, 1)

            def hidden(c, f):
                n = held(act, c + 1)
                wait(act, h_mm, n)
                A(h_hi[:, f % 2, :], h_bank[f % 2][:], ACT.Relu, bias=b1_cur[:, f:f + 1]).then_inc(h_hi_done, 1)
                A(h_full[:, f % 2, :], h_bank[f % 2][:], ACT.Relu, bias=b1_cur[:, f:f + 1]).then_inc(h_bank_free, 1)

            def ffn_block(s, att=True, last_att=False, last=False):
                b = sequence_of(act, s)
                b_next = None if last else sequence_of(act, s + 1)
                for f in range(FC):
                    c = FC * s + f
                    if att and f % 4 == 0:
                        parts = slot_parts(s + LEAD, f // 4, last_att and f == 12)
                    hidden(c, f)
                    if att:
                        parts[f % 4]()
                    if f + AHEAD < FC:
                        split_hi(c + AHEAD, f + AHEAD, b)
                    elif not last:
                        split_hi(c + AHEAD, f + AHEAD - FC, b_next)
                    if not last and f >= 8 and f % 2 == 0:
                        split_xn2T(s + 1, (f - 8) // 2)

            act.wait_ge(small_in, 16 * 8)
            A(gates[:], gates[:], ACT.Tanh).then_inc(gates_done, 1)
            for k in range(KD):
                act.wait_ge(setup_mm, k + 1)
                A(ctxT[:, k, :], bank[k][:], ACT.Copy).then_inc(setup_act, 1)
            for h in range(KD):
                act.wait_ge(setup_mm, KD + h + 1)
                A(kT[:, h, :], bank[h][:], ACT.Identity, bias=bk_sb[:, h:h + 1]).then_inc(setup_act, 1)
            for d in range(KD):
                act.wait_ge(setup_mm, 4 * KD + d + 1)
                A(m_all[:, d, :], bank[d][:], ACT.Copy).then_inc(setup_act, 1)

            act.wait_ge(setup_act, 3 * KD)
            act.sem_inc(out_bank_free, TPB)

            nc.scalar.preload_act_table_set("natural_log_exp_and_others")
            act.wait_ge(consts_done, 3)
            ln_root(1, 0)
            copy_xnT(1)
            for q in range(TPB):
                for part in slot_parts(0, q):
                    part()
            with loop(act, 1, LEAD) as m:
                for q in range(TPB):
                    for part in slot_parts(m, q):
                        part()

            for k in range(KD):
                split_xn2T(0, k)
            for f in range(AHEAD):
                split_hi(f, f, 0)
            with loop(act, 0, BLOCKS - LEAD - 1) as s:
                ffn_block(s)
            ffn_block(BLOCKS - LEAD - 1, last_att=True)
            copy_xn2T(TILES, 3, BLOCKS - 1)
            with loop(act, BLOCKS - LEAD, BLOCKS - 1) as s:
                ffn_block(s, att=False)
            ffn_block(BLOCKS - 1, att=False, last=True)

        @block.vector
        def _(dve):
            V = nc.vector

            def ln_stats(n, w, src):
                V.bn_stats(stats[w][:], src).then_inc(st_done[w], 1)

            def ln_aggregate(w):
                V.bn_aggr(mean_var[w][:], stats[w][:]).then_inc(mv_done[w], 1)

            def ln_apply(n, w, src, dst, done):
                wait(dve, ysq_done[w], n)
                V.scalar_tensor_tensor(out=newton[w][:], in0=mean_var[w][:, 1:2], scalar=EPS, in1=y_sq[w][:],
                                       op0=ALU.add, op1=ALU.mult).then_inc(newton_done[w], 1)
                wait(dve, newton_done[w], n)
                V.scalar_tensor_tensor(out=neg_rstd[w][:], in0=newton[w][:], scalar=S_NEWTON, in1=y_k[w][:],
                                       op0=ALU.subtract, op1=ALU.mult).then_inc(rstd_done[w], 1)
                wait(dve, rstd_done[w], n)
                V.tensor_scalar(dst, src, mean_var[w][:, 0:1], neg_rstd[w][:], ALU.subtract, ALU.mult).then_inc(done, 1)

            def slot_parts(m, q, last_tile=False):
                first = type(m) is int and m == 0 and q == 0
                n = held(dve, 4 * m + q + 1)
                keys = at(sequence_of(dve, m) * KEYS, KEYS)
                nx_q, prev_q = (q + 1) % 4, (q + 3) % 4

                def part0():
                    wait(dve, s_mm, n)
                    wait(dve, p_done, held(dve, n - 1))
                    V.scalar_tensor_tensor(out=neg_s[:], in0=bank_a[:, 0:KEYS], scalar=-1.0, in1=cb_all[:, keys],
                                           op0=ALU.mult, op1=ALU.subtract).then_inc(negs_done, 1)
                    if not last_tile:
                        wait(dve, x_loaded[nx_q], held(dve, 16 * (m + 1) if q < 3 else 16 * (m + 2)))
                        ln_stats(held(dve, n + 1), 0, x_ring[:, nx_q, :])
                        wait(dve, st_done[0], held(dve, n + 1))
                    wait(dve, negs_done, n)
                    V.tensor_reduce(neg_max[:], neg_s[:], AX_X, ALU.min).then_inc(s_read, 1)
                    if not last_tile:
                        ln_aggregate(0)
                    if not first:
                        wait(dve, xn2T_mm, held(dve, n - 2))
                        ln_apply(held(dve, n - 1), 1, x_ring[:, prev_q, :], xn2[:], xn2_done)

                def part1():
                    wait(dve, p_done, n)
                    V.reciprocal(p_inv[:], p_sum[:]).then_inc(pinv_done, 1)
                    if not last_tile:
                        wait(dve, xnT_mm, n)
                        ln_apply(held(dve, n + 1), 0, x_ring[:, nx_q, :], xn[:], xn_done)
                    wait(dve, pinv_done, n)
                    V.tensor_scalar(coef[:], p_inv[:], gate_x[:], NORM, ALU.mult, ALU.mult).then_inc(coef_done, 1)

                def part2():
                    wait(dve, o_mm, n)
                    wait(dve, coef_done, n)
                    V.scalar_tensor_tensor(out=x_ring[:, q, :], in0=bank_a[:], scalar=coef[:], in1=x_ring[:, q, :],
                                           op0=ALU.mult, op1=ALU.add).then_inc(x2_done, 1)
                    wait(dve, x2_done, n)
                    ln_stats(n, 1, x_ring[:, q, :])

                def part3():
                    wait(dve, st_done[1], n)
                    if not first:
                        token_sums(held(dve, n - 1), prev_q, (m - 1) if q == 0 else m)
                    ln_aggregate(1)
                    if q == 0 and not (type(m) is int and m == 0):
                        router(m)
                return part0, part1, part2, part3

            def token_sums(n, q, m):
                wait(dve, xn2T_done, n)
                in_seq = m % BPS if type(m) is int else nc.s_assert_within(dve.snap(m & (BPS - 1)), 0, BPS - 1, skip_runtime_bounds_check_because="the loop ends at a fixed block")
                col = at(in_seq * TPB + q, 1)
                V.reduce_sum(tok_sums[:, :, col], xn2T_st[:, q % 2], AX_X).then_inc(sum_done, 1)

            def router(m):
                wait(dve, sum_done, held(dve, 4 * m))
                V.reduce_sum(xsum[:], tok_sums[:], AX_X).then_inc(xsum_done, 1)
                mv = held(dve, m)
                wait(dve, router_mm, mv)
                V.scalar_tensor_tensor(out=logits[:], in0=bank_a[0:1, 0:EXPERTS], scalar=1.0 / SEQ, in1=br_sb[:],
                                       op0=ALU.mult, op1=ALU.add).then_inc(logits_done, 1)
                wait(dve, logits_done, mv)
                V.reduce_max(top[:], logits[:], AX_X).then_inc(top_done, 1)
                wait(dve, top_done, mv)
                V.scalar_tensor_tensor(out=reach[:], in0=logits[:], scalar=top[:], in1=rank_down[:],
                                       op0=ALU.is_ge, op1=ALU.mult).then_inc(reach_done, 1)
                wait(dve, reach_done, mv)
                V.reduce_max(best_rank[:], reach[:], AX_X).then_inc(rank_done, 1)
                wait(dve, rank_done, mv)
                V.tensor_scalar(expert[:, at(m, 1)], best_rank[:], -1.0, float(EXPERTS), ALU.mult, ALU.add).then_inc(expert_done, 1)

            def hidden_lo(c, f):
                wait(dve, h_bank_free, held(dve, c + 3))
                V.tensor_tensor(h_lo[:, f % 2, :], h_full[:, f % 2, :], h_hi[:, f % 2, :].bitcast(F32),
                                ALU.subtract).then_inc(h_lo_done, 1)

            def split_xn2T(s, k):
                wait(dve, xhi_done, held(dve, KD * s + k + 1))
                par = parity(dve, s)
                V.tensor_tensor(xn2T_lo[:, par, k, :].rearrange("p o (t n) -> p (o t) n", n=P), xn2T_raw[:, :, k, :],
                                xn2T_hi[:, par, k, :].rearrange("p o (t n) -> p (o t) n", n=P).bitcast(F32),
                                ALU.subtract).then_inc(xlo_done, 1)

            def add_b2(s, t):
                if t == 0:
                    wait(dve, x2_loaded, held(dve, 16 * s + 16))
                    wait(dve, b2_loaded, held(dve, 16 * (s // BPS + 1) if type(s) is int else 16 * ((s >> 2) + 1)))
                V.scalar_tensor_tensor(out=x2_blk[:, t, :], in0=b2_cur[:], scalar=gate_f[:], in1=x2_blk[:, t, :],
                                       op0=ALU.mult, op1=ALU.add).then_inc(b2_added, 1)

            def finish(s, t):
                if t < TPB - 1:
                    wait(dve, out_mm, held(dve, (TPB - 1) * s + t + 1))
                else:
                    wait(dve, w_slot_free, held(dve, RING + FC * s + FC))
                V.scalar_tensor_tensor(out=x2_blk[:, t, :], in0=out_bank[t][:], scalar=gate_f[:], in1=x2_blk[:, t, :],
                                       op0=ALU.mult, op1=ALU.add).then_inc(out_bank_free, 1)

            def ffn_block(s, att=True, last_att=False, last=False):
                for f in range(FC):
                    c = FC * s + f
                    if att and f % 4 == 0:
                        parts = slot_parts(s + LEAD, f // 4, last_att and f == 12)
                    hidden_lo(c, f)
                    if att:
                        parts[f % 4]()
                    if not last and f >= 8 and f % 2 == 0:
                        split_xn2T(s + 1, (f - 8) // 2)
                    if f >= 8 and f % 2 == 1:
                        add_b2(s, (f - 9) // 2)
                wait(dve, b2_added, held(dve, TPB * s + TPB))
                for t in range(TPB):
                    finish(s, t)

            V.memset(eps_c[:], EPS).then_inc(consts_done, 1)
            V.memset(lnk_c[:], LN_K).then_inc(consts_done, 1)
            V.memset(tok_sums[:], 0.0).then_inc(consts_done, 1)
            dve.wait_ge(small_in, 16 * 8)
            V.tensor_copy(bqb, bq_sb[:].rearrange("p (k o) -> p k o", o=1).to_broadcast([P, KD, P])).then_inc(consts_done, 1)
            dve.wait_ge(gates_done, 1)
            V.tensor_copy(gate_x[:], gates[:, 0:1])
            V.tensor_copy(gate_f[:], gates[:, 1:2]).then_inc(consts_done, 1)
            for h in range(KD):
                dve.wait_ge(setup_mm, 2 * KD + h + 1)
                V.tensor_copy(wqT[:, h, :], bank[4 + h][:]).then_inc(setup_dve, 1)
            for b in range(BATCH):
                dve.wait_ge(setup_mm, 3 * KD + b + 1)
                V.tensor_tensor(v_all[:, b, :], bank[4 + b][:], bv_sb, ALU.add).then_inc(setup_dve, 1)
            dve.wait_ge(setup_mm, 5 * KD + 1)
            V.tensor_copy(cb_all[:], bank[4][:]).then_inc(setup_dve, 1)
            dve.wait_ge(setup_dve, 2 * KD + 1)
            dve.sem_inc(h_bank_free, 2)
            dve.wait_ge(consts_done, 5)

            dve.wait_ge(x_loaded[0], 16)
            ln_stats(1, 0, x_ring[:, 0, :])
            dve.wait_ge(st_done[0], 1)
            ln_aggregate(0)
            ln_apply(1, 0, x_ring[:, 0, :], xn[:], xn_done)
            for q in range(TPB):
                for part in slot_parts(0, q):
                    part()
            with loop(dve, 1, LEAD) as m:
                for q in range(TPB):
                    for part in slot_parts(m, q):
                        part()

            for k in range(KD):
                split_xn2T(0, k)
            with loop(dve, 0, BLOCKS - LEAD - 1) as s:
                ffn_block(s)
            ffn_block(BLOCKS - LEAD - 1, last_att=True)
            ln_apply(TILES, 1, x_ring[:, 3, :], xn2[:], xn2_done)
            token_sums(TILES, 3, BLOCKS - 1)
            router(BLOCKS)
            with loop(dve, BLOCKS - LEAD, BLOCKS - 1) as s:
                ffn_block(s, att=False)
            ffn_block(BLOCKS - 1, att=False, last=True)

        @block.gpsimd
        def _(pool):
            with loop(pool, 0, BLOCKS) as s:
                for f in range(FC):
                    wait(pool, w_hi_done, held(pool, FC * s + f + 1))
                    nc.gpsimd.tensor_tensor(w_lo[:, f % RING, :], w_raw[:, f, 0:2 * D],
                                            w_hi[:, f % RING, :].bitcast(F32), ALU.subtract)
                    nc.gpsimd.tensor_copy(b1_cur[:, f:f + 1], w_raw[:, f, 2 * D:2 * D + 1]).then_inc(w_lo_done, 1)


LN_K = -0.23104906018664842

_INS = ["x", "ctx_1024", "g_xattn", "g_ffn", "L0_xattn_Wq", "L0_xattn_bq", "L0_xattn_Wk", "L0_xattn_bk",
        "L0_xattn_Wv", "L0_xattn_bv", "L0_ffn_Wr", "L0_ffn_br", "L0_ffn_W1", "L0_ffn_b1", "L0_ffn_W2", "L0_ffn_b2"]


def kernel(**inputs):
    import numpy as np
    import concourse.bacc as bacc
    from concourse.bass_utils import run_bass_kernel_spmd

    nc = bacc.Bacc("TRN2", target_bir_lowering=False, num_devices=1)
    arrays, args = {}, []
    for name in _INS:
        a = np.ascontiguousarray(inputs[name])
        if name == "x":
            a = a.reshape(BLOCKS, TPB, P, D)
        arrays[f"in_{name}"] = a
        args.append(nc.dram_tensor(f"in_{name}", a.shape, mybir.dt.from_np(a.dtype), kind="ExternalInput").ap())
    arrays["identity"] = np.eye(P, dtype=np.float32)
    args.append(nc.dram_tensor("identity", (P, P), F32, kind="ExternalInput").ap())
    arrays["rank_down"] = np.arange(EXPERTS, 0, -1, dtype=np.float32)[None, :]
    args.append(nc.dram_tensor("rank_down", (1, EXPERTS), F32, kind="ExternalInput").ap())
    out = nc.dram_tensor("out", (BLOCKS, TPB, P, D), F32, kind="ExternalOutput").ap()
    gated_block(nc, *args, out.rearrange("s t p n -> s p t n"))
    got = run_bass_kernel_spmd(nc, [arrays], core_ids=[0])
    return got.results[0]["out"].reshape(BATCH, SEQ, D)
```

```python
from contextlib import ExitStack

import concourse.bass as bass
from concourse import mybir

F32 = mybir.dt.float32
F32R = mybir.dt.float32r
U32 = mybir.dt.uint32
ALU = mybir.AluOpType
ACT = mybir.ActivationFunctionType
AX_X = mybir.AxisListType.X

P = 128
BATCH, SEQ, D = 4, 2048, 512
KEYS = 128
HIDDEN = 2048
EXPERTS = 8
KD = D // P
ROWS = 512
TPB = ROWS // P
BLOCKS = BATCH * SEQ // ROWS
BPS = SEQ // ROWS
TILES = BLOCKS * TPB
TPS = SEQ // P
FC = HIDDEN // P
LEAD = BPS + 1
RING = 4
AHEAD = 3
EPS = 1e-5
NORM = float(D) ** -0.5
BIG = 3.0e38
K_NEWTON = 0.5 ** (1.0 / 3.0)
S_NEWTON = 3.0 * K_NEWTON * K_NEWTON


def gated_block(nc, x, ctx_in, g_xattn, g_ffn, wq, bq, wk, bk, wv, bv, wr, br, w1, b1, w2, b2, ident_in, rank_in, out):
    ctx = ExitStack()
    with ctx:
        def sb(name, shape, dt=F32):
            return ctx.enter_context(nc.sbuf_tensor(name, shape, dt))

        def sem(name):
            return ctx.enter_context(nc.semaphore(name))

        x2_dram = nc.dram_tensor("x2_dram", (TILES, P, D), F32, kind="Internal").ap()
        xn2T_dram = nc.dram_tensor("xn2T_dram", (TILES, P, KD, P), F32, kind="Internal").ap()

        w_raw = sb("w_raw", [P, FC, 2 * D + 1])
        w_hi = sb("w_hi", [P, RING, 2 * D], F32R)
        w_lo = sb("w_lo", [P, RING, 2 * D], F32R)
        b1_cur = sb("b1_cur", [P, FC])
        b2_cur = sb("b2_cur", [P, D])
        xn2T_raw = sb("xn2T_raw", [P, TPB, KD, P])
        xn2T_hi = sb("xn2T_hi", [P, 2, KD, ROWS], F32R)
        xn2T_lo = sb("xn2T_lo", [P, 2, KD, ROWS], F32R)
        x2_blk = sb("x2_blk", [P, TPB, D])
        h_full = sb("h_full", [P, 2, ROWS])
        h_hi = sb("h_hi", [P, 2, ROWS], F32R)
        h_lo = sb("h_lo", [P, 2, ROWS], F32R)
        m_all = sb("m_all", [P, KD, BATCH * KEYS])
        v_all = sb("v_all", [P, BATCH, D])
        cb_all = sb("cb_all", [P, BATCH * KEYS])
        ident = sb("ident", [P, P])
        wr_sb = sb("wr_sb", [P, KD, EXPERTS])
        br_sb = sb("br_sb", [1, EXPERTS])
        gates = sb("gates", [P, 2])
        gate_x = sb("gate_x", [P, 1])
        gate_f = sb("gate_f", [P, 1])
        eps_c = sb("eps_c", [P, 1])
        lnk_c = sb("lnk_c", [P, 1])
        bk_sb = sb("bk_sb", [P, KD])
        bq_sb = sb("bq_sb", [P, KD])
        x_ring = sb("x_ring", [P, 4, D])
        xn = sb("xn", [P, D])
        xnT = sb("xnT", [P, KD, P])
        neg_s = sb("neg_s", [P, KEYS])
        neg_max = sb("neg_max", [P, 1])
        probs = sb("probs", [P, KEYS])
        p_sum = sb("p_sum", [P, 1])
        p_inv = sb("p_inv", [P, 1])
        coef = sb("coef", [P, 1])
        pT = sb("pT", [P, P])
        xn2 = sb("xn2", [P, D])
        xn2T_st = sb("xn2T_st", [P, 2, KD, P])
        tok_sums = sb("tok_sums", [P, KD, TPS])
        stats = [sb(f"stats{n}", [P, 6]) for n in (1, 2)]
        mean_var = sb("mean_var", [P, 2, 2])
        ln_v, y_k, y_sq, newton, neg_rstd = (sb(n, [P, 2]) for n in ("ln_v", "y_k", "y_sq", "newton", "neg_rstd"))
        xsum = sb("xsum", [P, KD])
        logits = sb("logits", [1, EXPERTS])
        rank_down = sb("rank_sb", [1, EXPERTS])
        top = sb("top", [1, 1])
        reach = sb("reach", [1, EXPERTS])
        best_rank = sb("best_rank", [1, 1])
        expert = sb("expert", [1, BLOCKS + 1], U32)

        def in_w(at, n):
            per = (2 * D + 1) * FC
            flat = w_raw[:].rearrange("p f n -> p (f n)")
            assert (at + 1) * KD * D <= per
            return flat[:, at * KD * D:at * KD * D + KD * n].rearrange("p (k n) -> p k n", k=KD)

        wk_sb, wq_sb, wv_sb, wqT = (in_w(i, D) for i in range(4))
        bqb, ctxT, kT = in_w(4, P), in_w(5, P), in_w(6, P)
        ctx_seq = in_w(7, P).rearrange("p k n -> p (k n)")
        bv_sb = x2_blk[:, 0, :]

        bank = [ctx.enter_context(nc.psum_tensor(f"bank{i}", [P, 512], F32)) for i in range(8)]
        out_bank = bank[0:4]
        h_bank = bank[4:6]
        BESIDE = dict(s=bank[6], pT=bank[6], o=bank[6], xnT=bank[7], xn2T=bank[7])
        ALONE = dict(s=bank[6], pT=bank[5], o=bank[4], xnT=bank[7], xn2T=bank[3])
        router_bank = bank[7]

        ident_in_sem, wk_in, wq_in, wv_in, small_in = (sem(n) for n in ("ident_in", "wk_in", "wq_in", "wv_in", "small_in"))
        wqT_mm, wqT_act, wqT_dve, consts_done = (sem(n) for n in ("wqT_mm", "wqT_act", "wqT_dve", "consts_done"))
        ctx_loaded, ctxT_mm, ctxT_done = sem("ctx_loaded"), sem("ctxT_mm"), sem("ctxT_done")
        k_mm, k_done, m_mm, m_done = (sem(n) for n in ("k_mm", "k_done", "m_mm", "m_done"))
        v_mm, v_done, cb_mm, cb_done = (sem(n) for n in ("v_mm", "v_done", "cb_mm", "cb_done"))
        gates_done = sem("gates_done")
        x_loaded = [sem(f"x_loaded{i}") for i in range(4)]
        x2_stored = [sem(f"x2_stored{i}") for i in range(4)]
        xn2T_stored = [sem(f"xn2T_stored{i}") for i in range(2)]
        st_done = [sem(f"st_done{n}") for n in (1, 2)]
        mv_done, lnv_done, yk_done, ysq_done, newton_done, rstd_done = (
            sem(n) for n in ("mv_done", "lnv_done", "yk_done", "ysq_done", "newton_done", "rstd_done"))
        xn_done, xnT_mm, xnT_done = sem("xn_done"), sem("xnT_mm"), sem("xnT_done")
        s_mm, negs_done, s_read, p_done = (sem(n) for n in ("s_mm", "negs_done", "s_read", "p_done"))
        pT_mm, pT_done = sem("pT_mm"), sem("pT_done")
        pinv_done, coef_done, o_mm, x2_done = (sem(n) for n in ("pinv_done", "coef_done", "o_mm", "x2_done"))
        xn2_done, xn2T_mm, xn2T_done, sum_done = (sem(n) for n in ("xn2_done", "xn2T_mm", "xn2T_done", "sum_done"))
        xsum_done, router_mm, logits_done, top_done, reach_done, rank_done, expert_done = (
            sem(n) for n in ("xsum_done", "router_mm", "logits_done", "top_done", "reach_done", "rank_done", "expert_done"))
        w_loaded = [sem(f"w_loaded{f}") for f in range(FC)]
        b2_loaded = sem("b2_loaded")
        w_hi_done, w_lo_done, w_slot_free = sem("w_hi_done"), sem("w_lo_done"), sem("w_slot_free")
        xn2T_loaded, x2_loaded, out_stored = sem("xn2T_loaded"), sem("x2_loaded"), sem("out_stored")
        xhi_done, xlo_done = sem("xhi_done"), sem("xlo_done")
        h_mm, h_bank_free, h_hi_done, h_lo_done = (sem(n) for n in ("h_mm", "h_bank_free", "h_hi_done", "h_lo_done"))
        b2_added, out_mm, out_bank_free = sem("b2_added"), sem("out_mm"), sem("out_bank_free")

        def rows_of(w):
            return w.rearrange("(k p) n -> p k n", p=P)

        def loop(eng, lo, hi):
            return nc.Fori(lo, hi, engines=[eng.engine], hint_back_edge=True)

        def held(eng, v):
            return v if type(v) is int else eng.snap(eng.to_reg(v) if eng.engine == mybir.EngineType.SP else v)

        def wait(eng, s, v):
            if type(v) is not int or v > 0:
                eng.wait_ge(s, v)

        def sequence_of(eng, blk):
            return blk // BPS if type(blk) is int else nc.s_assert_within(eng.snap(blk >> 2), 0, BATCH - 1, skip_runtime_bounds_check_because="the loop ends at a fixed block")

        def parity(eng, blk):
            return at(blk % 2 if type(blk) is int else nc.s_assert_within(eng.snap(blk & 1), 0, 1, skip_runtime_bounds_check_because="the loop ends at a fixed block"), 1)

        def at(start, size):
            return slice(start, start + size) if type(start) is int else bass.ds(start, size)

        block = ctx.enter_context(nc.Block())

        @block.sync
        def _(sp):
            x2_blocks = x2_dram.rearrange("(s t) p n -> s p t n", t=TPB)
            xn2T_blocks = xn2T_dram.rearrange("(s t) p k n -> s p t k n", t=TPB)

            def load_x(m, q):
                sp.dma_start(x_ring[:, q, :], x[m, q]).then_inc(x_loaded[q], 16)

            def store_x2(m, q):
                n = held(sp, 4 * m + q + 1)
                wait(sp, x2_done, n)
                sp.dma_start(x2_dram[n - 1], x_ring[:, q, :]).then_inc(x2_stored[q], 16)

            def store_xn2T(m, q):
                n = held(sp, 4 * m + q + 1)
                wait(sp, xn2T_done, n)
                sp.dma_start(xn2T_dram[n - 1], xn2T_st[:, q % 2]).then_inc(xn2T_stored[q % 2], 16)

            def stores(m, q):
                first = type(m) is int and m == 0
                if q > 0:
                    store_x2(m, q - 1)
                elif not first:
                    store_x2(m - 1, 3)
                if q > 1:
                    store_xn2T(m, q - 2)
                elif not first:
                    store_xn2T(m - 1, q + 2)

            def load_ahead(m, q, last=False):
                if type(m) is int and m == 0 and q == 0:
                    load_x(m, 3)
                elif q == 0 or not last:
                    stored, normed = held(sp, 16 * (m + 1) if q else 16 * m), held(sp, 4 * m + q)
                    wait(sp, x2_stored[(q + 3) % 4], stored)
                    wait(sp, xn2_done, normed)
                    if q == 0:
                        load_x(m, 3)
                    else:
                        load_x(m + 1, q - 1)

            def load_ctx(b):
                wait(sp, ctxT_mm, held(sp, b))
                sp.dma_start(ctx_seq, ctx_in[b]).then_inc(ctx_loaded, 16)

            def load_chunks(e, f0, f1, used):
                for f in range(f0, f1):
                    if used is not None:
                        wait(sp, w_lo_done, held(sp, used + f + 1))
                    cols = slice(f * P, (f + 1) * P)
                    sp.dma_start(w_raw[:, f, 0:D].rearrange("p (k n) -> p k n", k=KD),
                                 w1[bass.ds(e, 1), :, cols].rearrange("e (k p) n -> p (e k) n", p=P)).then_inc(w_loaded[f], 16)
                    sp.dma_start(w_raw[:, f, D:2 * D], w2[bass.ds(e, 1), cols, :].rearrange("e p n -> p (e n)")).then_inc(w_loaded[f], 16)
                    with nc.allow_non_contiguous_dma(reason="one bias per partition"):
                        sp.dma_start(w_raw[:, f, 2 * D:2 * D + 1],
                                     b1[bass.ds(e, 1), cols].rearrange("e p -> p e")).then_inc(w_loaded[f], 16)

            def load_b2(e, used):
                if used is not None:
                    wait(sp, b2_added, held(sp, used))
                sp.dma_start(b2_cur[:], b2[bass.ds(e, 1), :].rearrange("e n -> (e n)").partition_broadcast(P)).then_inc(b2_loaded, 16)

            def chosen(m):
                wait(sp, expert_done, held(sp, m))
                return sp.value_load(expert[0:1, m:m + 1], min_val=0, max_val=EXPERTS - 1)

            def load_xn2T(s):
                stored, split = held(sp, 32 * s + 32), held(sp, KD * s)
                for par in range(2):
                    wait(sp, xn2T_stored[par], stored)
                wait(sp, xhi_done, split)
                wait(sp, xlo_done, split)
                sp.dma_start(xn2T_raw[:], xn2T_blocks[s]).then_inc(xn2T_loaded, 16)

            def store_out(s):
                wait(sp, out_bank_free, held(sp, 4 * s + 8))
                sp.dma_start(out[s], x2_blk[:]).then_inc(out_stored, 16)

            def load_x2(s):
                stored, free = held(sp, 16 * s + 16), held(sp, 16 * s)
                for q in range(TPB):
                    wait(sp, x2_stored[q], stored)
                wait(sp, out_stored, free)
                sp.dma_start(x2_blk[:], x2_blocks[s]).then_inc(x2_loaded, 16)

            def ffn_block(s, att=True, last_att=False, switch=False, closing=False):
                if att:
                    stores(s + LEAD, 0)
                if closing:
                    store_x2(BLOCKS - 1, 3)
                    store_xn2T(BLOCKS - 1, 2)
                if not (type(s) is int and s == 0):
                    store_out(s - 1)
                if type(s) is not int or s < BLOCKS - 1:
                    load_xn2T(s + 1)
                load_x2(s)
                if att:
                    load_ahead(s + LEAD, 0, last_att)
                    stores(s + LEAD, 1)
                if closing:
                    store_xn2T(BLOCKS - 1, 3)
                if switch:
                    e = chosen(s + LEAD)
                    load_chunks(e, 0, 4, FC * s)
                if att:
                    load_ahead(s + LEAD, 1, last_att)
                for q in range(2, TPB):
                    if att:
                        stores(s + LEAD, q)
                    if switch:
                        load_chunks(e, 4 * q - 4, 4 * q, FC * s)
                    if att:
                        load_ahead(s + LEAD, q, last_att)
                if switch:
                    load_chunks(e, 12, 16, FC * s)
                    load_b2(e, 4 * s + 4)

            sp.dma_start(ident[:], ident_in).then_inc(ident_in_sem, 16)
            load_ctx(0)
            sp.dma_start(wk_sb, rows_of(wk)).then_inc(wk_in, 16)
            load_x(0, 0)
            with nc.allow_non_contiguous_dma(reason="small vectors, one value per partition"):
                sp.dma_start(bk_sb[:], bk.rearrange("(k p) -> p k", p=P)).then_inc(small_in, 16)
                sp.dma_start(bq_sb[:], bq.rearrange("(k p) -> p k", p=P)).then_inc(small_in, 16)
            sp.dma_start(wq_sb, rows_of(wq)).then_inc(wq_in, 16)
            load_x(0, 1)
            sp.dma_start(bv_sb, bv.partition_broadcast(P)).then_inc(small_in, 16)
            sp.dma_start(gates[:, 0:1], g_xattn.partition_broadcast(P)).then_inc(small_in, 16)
            sp.dma_start(gates[:, 1:2], g_ffn.partition_broadcast(P)).then_inc(small_in, 16)
            sp.dma_start(wr_sb[:], rows_of(wr)).then_inc(small_in, 16)
            sp.dma_start(br_sb[:], br[None, :]).then_inc(small_in, 16)
            sp.dma_start(rank_down[:], rank_in).then_inc(small_in, 16)
            sp.dma_start(wv_sb, rows_of(wv)).then_inc(wv_in, 16)
            load_x(0, 2)

            for q in range(TPB):
                stores(0, q)
                load_ahead(0, q)
            with loop(sp, 1, BATCH) as m:
                load_ctx(m)
                for q in range(TPB):
                    stores(m, q)
                    load_ahead(m, q)
            stores(LEAD - 1, 0)
            load_xn2T(0)
            load_ahead(LEAD - 1, 0)
            stores(LEAD - 1, 1)
            load_ahead(LEAD - 1, 1)
            e = chosen(LEAD - 1)
            load_chunks(e, 0, 3, None)
            stores(LEAD - 1, 2)
            load_ahead(LEAD - 1, 2)
            load_chunks(e, 3, 6, None)
            stores(LEAD - 1, 3)
            load_ahead(LEAD - 1, 3)
            load_chunks(e, 6, FC, None)
            load_b2(e, None)

            ffn_block(0)
            with loop(sp, 1, 3) as s:
                ffn_block(s)
            ffn_block(3, switch=True)
            with loop(sp, 4, 7) as s:
                ffn_block(s)
            ffn_block(7, switch=True)
            with loop(sp, 8, 10) as s:
                ffn_block(s)
            ffn_block(10, last_att=True)
            ffn_block(11, att=False, switch=True, closing=True)
            with loop(sp, 12, 15) as s:
                ffn_block(s, att=False)
            ffn_block(15, att=False)
            store_out(15)
            sp.wait_ge(out_stored, 16 * BLOCKS)
            for q in range(4):
                sp.wait_ge(x2_stored[q], 16 * BLOCKS)
            for par in range(2):
                sp.wait_ge(xn2T_stored[par], 32 * BLOCKS)

        @block.tensor
        def _(pe):
            def mm(dst, lhsT, rhs, start, stop):
                return pe.matmul(dst, lhsT, rhs, start=start, stop=stop)

            def transpose_xn(n, bk, q, m):
                wait(pe, xn_done, n)
                if bk is BESIDE:
                    wait(pe, xn2T_done, held(pe, n - 2))
                elif q == 2:
                    wait(pe, logits_done, held(pe, m))
                for k in range(KD):
                    last = pe.transpose(bk["xnT"][:, k * P:(k + 1) * P], xn[:, k * P:(k + 1) * P], ident[:])
                last.then_inc(xnT_mm, 1)

            def scores(n, bk, b, q):
                wait(pe, xnT_done, n)
                if bk is BESIDE:
                    wait(pe, x2_done, held(pe, n - 1))
                if q == 0:
                    wait(pe, m_done, held(pe, b + 1))
                for k in range(KD):
                    last = mm(bk["s"][:, 0:KEYS], xnT[:, k, :], m_all[:, k, at(b * KEYS, KEYS)], k == 0, k == KD - 1)
                last.then_inc(s_mm, 1)

            def transpose_p(n, bk):
                wait(pe, p_done, n)
                pe.transpose(bk["pT"][:, 0:P], probs[:], ident[:]).then_inc(pT_mm, 1)

            def attend(n, bk, b, q):
                wait(pe, pT_done, n)
                if bk is ALONE:
                    wait(pe, x2_done, held(pe, n - 1))
                if q == 0:
                    wait(pe, v_done, held(pe, b + 1))
                mm(bk["o"][:], pT[:], v_all[:, at(b, 1), :].rearrange("p o n -> p (o n)"), True, True).then_inc(o_mm, 1)

            def transpose_xn2(n, bk, q=0, m=0):
                wait(pe, xn2_done, n)
                if bk is ALONE:
                    wait(pe, xn2T_done, held(pe, n - 1))
                elif q == 1:
                    wait(pe, logits_done, held(pe, m))
                for k in range(KD):
                    last = pe.transpose(bk["xn2T"][:, k * P:(k + 1) * P], xn2[:, k * P:(k + 1) * P], ident[:])
                last.then_inc(xn2T_mm, 1)

            def router(m):
                wait(pe, xsum_done, held(pe, m))
                for k in range(KD):
                    last = mm(router_bank[0:1, 0:EXPERTS], xsum[:, k:k + 1], wr_sb[:, k, :], k == 0, k == KD - 1)
                last.then_inc(router_mm, 1)

            def slot_parts(m, q, bk):
                o_bk = BESIDE if type(m) is int and m == LEAD - 1 and q == TPB - 1 else bk
                n = held(pe, 4 * m + q + 1)
                b = sequence_of(pe, m)

                def part0():
                    transpose_xn(n, bk, q, m)

                def part1():
                    scores(n, bk, b, q)

                def part2():
                    transpose_p(n, bk)
                    if q == 1 and not (type(m) is int and m == 0):
                        router(m)

                def part3():
                    attend(n, o_bk, b, q)

                def part4():
                    if not (type(m) is int and m == 0 and q == 0):
                        transpose_xn2(held(pe, n - 1), bk, q, m)
                return part0, part1, part2, part3, part4

            def ctx_transpose(b):
                wait(pe, ctx_loaded, held(pe, 16 * b + 16))
                wait(pe, v_done, held(pe, b))
                for k in range(KD):
                    last = pe.transpose(bank[0][:, k * P:(k + 1) * P], ctx_seq[:, k * P:(k + 1) * P], ident[:])
                last.then_inc(ctxT_mm, 1)

            def keys_part(b, h0, h1):
                if h0 == 0:
                    wait(pe, ctxT_done, held(pe, b + 1))
                    wait(pe, cb_done, held(pe, b))
                for h in range(h0, h1):
                    for k in range(KD):
                        last = mm(bank[1][:, h * P:(h + 1) * P], wk_sb[:, k, h * P:(h + 1) * P], ctxT[:, k, :], k == 0, k == KD - 1)
                if h1 == KD:
                    last.then_inc(k_mm, 1)

            def values_part(b, k0, k1):
                for k in range(k0, k1):
                    last = mm(bank[0][:], ctxT[:, k, :], wv_sb[:, k, :], k == 0, k == KD - 1)
                if k1 == KD:
                    last.then_inc(v_mm, 1)

            def folded_part(b, d0, d1):
                if d0 == 0:
                    wait(pe, k_done, held(pe, b + 1))
                    wait(pe, m_done, held(pe, b))
                for d in range(d0, d1):
                    for h in range(KD):
                        last = mm(bank[2][:, d * P:(d + 1) * P], wqT[:, h, d * P:(d + 1) * P], kT[:, h, :], h == 0, h == KD - 1)
                if d1 == KD:
                    last.then_inc(m_mm, 1)

            def bias_scores(b):
                for h in range(KD):
                    last = mm(bank[1][:, 0:KEYS], bqb[:, h, :], kT[:, h, :], h == 0, h == KD - 1)
                last.then_inc(cb_mm, 1)

            def attention_block(m, with_keys):
                units = [lambda: ctx_transpose(m)]
                units += [lambda h=h: keys_part(m, h, h + 1) for h in range(KD)]
                units += [lambda k=k: values_part(m, k, k + 1) for k in range(KD)]
                units += [lambda d=d: folded_part(m, d, d + 1) for d in range(KD)]
                units += [lambda: bias_scores(m)]

                def gap(n):
                    for unit in units[:n] if with_keys else []:
                        unit()
                    del units[:n]
                for q in range(TPB):
                    part0, part1, part2, part3, part4 = slot_parts(m, q, ALONE)
                    part0()
                    gap(1)
                    part1()
                    gap(2)
                    part2()
                    part3()
                    gap(1)
                    part4()

            def ffn_up(c, f, xs):
                wait(pe, w_lo_done, held(pe, c + 1))
                wait(pe, h_bank_free, held(pe, c + 1))
                dst, slot = h_bank[f % 2][:], f % RING
                for k in range(KD):
                    hi = w_hi[:, slot, k * P:(k + 1) * P]
                    lo = w_lo[:, slot, k * P:(k + 1) * P]
                    mm(dst, hi, xn2T_hi[:, xs, k, :].rearrange("p o n -> p (o n)"), k == 0, False)
                    mm(dst, hi, xn2T_lo[:, xs, k, :].rearrange("p o n -> p (o n)"), False, False)
                    last = mm(dst, lo, xn2T_hi[:, xs, k, :].rearrange("p o n -> p (o n)"), False, k == KD - 1)
                last.then_inc(h_mm, 1)

            def ffn_down(c, f):
                slot = f % RING
                whi, wlo = w_hi[:, slot, D:2 * D], w_lo[:, slot, D:2 * D]
                n = held(pe, c + 1)
                wait(pe, h_hi_done, n)
                for t in range(TPB):
                    if f == 0:
                        wait(pe, out_bank_free, held(pe, 4 * (c // FC) + t + 1 if type(c) is int else (c >> 2) + t + 1))
                    cols = slice(t * P, (t + 1) * P)
                    mm(out_bank[t][:], h_hi[:, f % 2, cols], whi, f == 0, False)
                    mm(out_bank[t][:], h_hi[:, f % 2, cols], wlo, False, False)
                wait(pe, h_lo_done, n)
                for t in range(TPB):
                    last = mm(out_bank[t][:], h_lo[:, f % 2, t * P:(t + 1) * P], whi, False, f == FC - 1)
                    if f == FC - 1 and t < TPB - 1:
                        last.then_inc(out_mm, 1)
                last.then_inc(w_slot_free, 1)

            def ffn_block(s, att=True, closing=False):
                xs = parity(pe, s)
                wait(pe, xlo_done, held(pe, KD * s + KD))
                for f in range(FC):
                    c = FC * s + f
                    if att and f % 4 == 0:
                        parts = slot_parts(s + LEAD, f // 4, BESIDE)
                    ffn_up(c, f, xs)
                    if f > 0:
                        ffn_down(c - 1, f - 1)
                    if att:
                        parts[f % 4]()
                        if f % 4 == 3:
                            parts[4]()
                    if closing and f == 3:
                        transpose_xn2(TILES, BESIDE)
                    if closing and f == 6:
                        wait(pe, xn2T_done, TILES)
                        router(BLOCKS)
                ffn_down(FC * s + FC - 1, FC - 1)

            pe.wait_ge(ident_in_sem, 16)
            ctx_transpose(0)
            pe.wait_ge(wk_in, 16)
            keys_part(0, 0, KD)
            pe.wait_ge(wq_in, 16)
            for h in range(KD):
                for k in range(KD):
                    last = pe.transpose(bank[3 + h][:, k * P:(k + 1) * P], wq_sb[:, k, h * P:(h + 1) * P], ident[:])
                last.then_inc(wqT_mm, 1)
            pe.sem_inc(w_slot_free, RING)
            pe.wait_ge(wqT_act, 2)
            pe.wait_ge(wqT_dve, 2)
            folded_part(0, 0, KD)
            pe.wait_ge(consts_done, 4)
            bias_scores(0)
            pe.wait_ge(wv_in, 16)
            values_part(0, 0, KD)

            attention_block(0, False)
            with loop(pe, 1, BATCH) as m:
                attention_block(m, True)
            attention_block(LEAD - 1, False)

            lead_tiles = LEAD * TPB
            pe.wait_ge(cb_done, BATCH)
            pe.wait_ge(m_done, BATCH)
            pe.wait_ge(v_done, BATCH)
            pe.wait_ge(xn2T_done, lead_tiles - 1)
            pe.wait_ge(pT_done, lead_tiles)
            pe.wait_ge(x2_done, lead_tiles - 1)
            pe.sem_inc(h_bank_free, 2)
            pe.sem_inc(out_bank_free, TPB)

            with loop(pe, 0, BLOCKS - LEAD) as s:
                ffn_block(s)
            ffn_block(BLOCKS - LEAD, att=False, closing=True)
            with loop(pe, BLOCKS - LEAD + 1, BLOCKS) as s:
                ffn_block(s, att=False)

        @block.scalar
        def _(act):
            A = nc.scalar.activation

            def ln_v_of(r):
                wait(act, mv_done, r)
                A(ln_v[:], mean_var[:, :, 1], ACT.Ln, bias=eps_c[:]).then_inc(lnv_done, 1)

            def inverse_roots(r):
                wait(act, lnv_done, r)
                A(y_k[:], ln_v[:], ACT.Exp, bias=lnk_c[:], scale=-0.5).then_inc(yk_done, 1)
                wait(act, yk_done, r)
                A(y_sq[:], y_k[:], ACT.Square).then_inc(ysq_done, 1)

            def exp_scores(n):
                wait(act, s_read, n)
                A(probs[:], neg_s[:], ACT.Exp, bias=neg_max[:], scale=-1.0, accum_out=p_sum[:]).then_inc(p_done, 1)

            def copy_pT(n, bk):
                wait(act, pT_mm, n)
                wait(act, o_mm, held(act, n - 1))
                A(pT[:], bk["pT"][:, 0:P], ACT.Copy).then_inc(pT_done, 1)

            def copy_xnT(n, bk):
                wait(act, xnT_mm, n)
                wait(act, s_mm, held(act, n - 1))
                A(xnT[:].rearrange("p k n -> p (k n)"), bk["xnT"][:], ACT.Copy, scale=-1.0).then_inc(xnT_done, 1)

            def copy_xn2T(n, q, m, bk):
                wait(act, xn2T_mm, n)
                wait(act, xn2T_stored[q % 2], held(act, 32 * m + 16 * (q // 2)))
                wait(act, sum_done, held(act, n - 2))
                A(xn2T_st[:, q % 2].rearrange("p k n -> p (k n)"), bk["xn2T"][:], ACT.Copy, scale=-1.0).then_inc(xn2T_done, 1)

            def slot_parts(m, q, bk):
                first = type(m) is int and m == 0 and q == 0
                n = held(act, 4 * m + q + 1)

                def part0():
                    copy_xnT(n, bk)

                def part1():
                    r = held(act, n + 1)
                    ln_v_of(r)
                    exp_scores(n)
                    inverse_roots(r)

                def part2():
                    copy_pT(n, bk)

                def part3():
                    if not first:
                        if q > 0:
                            copy_xn2T(held(act, n - 1), q - 1, m, bk)
                        else:
                            copy_xn2T(held(act, n - 1), 3, m - 1, bk)
                return part0, part1, part2, part3

            def copy_ctxT(b):
                wait(act, ctxT_mm, held(act, b + 1))
                A(ctxT.rearrange("p k n -> p (k n)"), bank[0][:], ACT.Copy).then_inc(ctxT_done, 1)

            def copy_folded(b):
                wait(act, m_mm, held(act, b + 1))
                A(m_all[:, :, at(b * KEYS, KEYS)], bank[2][:].rearrange("p (k n) -> p k n", k=KD), ACT.Copy).then_inc(m_done, 1)

            def copy_bias(b):
                wait(act, cb_mm, held(act, b + 1))
                A(cb_all[:, at(b * KEYS, KEYS)], bank[1][:, 0:KEYS], ACT.Copy).then_inc(cb_done, 1)

            def split_hi(c, f, b):
                wait(act, w_loaded[f], held(act, 48 * b + 48))
                wait(act, w_slot_free, held(act, c + 1))
                A(w_hi[:, f % RING, :], w_raw[:, f, 0:2 * D], ACT.Copy).then_inc(w_hi_done, 1)

            def split_xn2T(s, k):
                if k == 0:
                    wait(act, xn2T_loaded, held(act, 16 * s + 16))
                par = parity(act, s)
                A(xn2T_hi[:, par, k, :].rearrange("p o (t n) -> p (o t) n", n=P), xn2T_raw[:, :, k, :], ACT.Copy).then_inc(xhi_done, 1)

            def hidden(c, f):
                n = held(act, c + 1)
                wait(act, h_mm, n)
                A(h_hi[:, f % 2, :], h_bank[f % 2][:], ACT.Relu, bias=b1_cur[:, f:f + 1]).then_inc(h_hi_done, 1)
                A(h_full[:, f % 2, :], h_bank[f % 2][:], ACT.Relu, bias=b1_cur[:, f:f + 1]).then_inc(h_bank_free, 1)

            def ffn_block(s, att=True, last=False, closing=False):
                b = sequence_of(act, s)
                b_next = None if last else sequence_of(act, s + 1)
                for f in range(FC):
                    c = FC * s + f
                    if att and f % 4 == 0:
                        parts = slot_parts(s + LEAD, f // 4, BESIDE)
                    hidden(c, f)
                    if att:
                        parts[f % 4]()
                    if closing and f == 1:
                        ln_v_of(TILES + 2)
                        inverse_roots(TILES + 2)
                    if closing and f == 3:
                        copy_xn2T(TILES, 3, BLOCKS - 1, BESIDE)
                    if f + AHEAD < FC:
                        split_hi(c + AHEAD, f + AHEAD, b)
                    elif not last:
                        split_hi(c + AHEAD, f + AHEAD - FC, b_next)
                    if not last and f >= 8 and f % 2 == 0:
                        split_xn2T(s + 1, (f - 8) // 2)

            copy_ctxT(0)
            act.wait_ge(small_in, 16 * 8)
            A(gates[:], gates[:], ACT.Tanh).then_inc(gates_done, 1)
            for h in (0, 2):
                act.wait_ge(wqT_mm, h + 1)
                A(wqT[:, h, :], bank[3 + h][:], ACT.Copy).then_inc(wqT_act, 1)
            nc.scalar.preload_act_table_set("natural_log_exp_and_others")
            act.wait_ge(consts_done, 3)
            ln_v_of(1)
            inverse_roots(1)
            copy_folded(0)
            copy_bias(0)

            for q in range(TPB):
                for part in slot_parts(0, q, ALONE):
                    part()
            with loop(act, 1, BATCH) as m:
                for q in range(TPB):
                    part0, part1, part2, part3 = slot_parts(m, q, ALONE)
                    part0()
                    if q == 0:
                        copy_ctxT(m)
                    part1()
                    part2()
                    part3()
                    if q == 3:
                        copy_folded(m)
                        copy_bias(m)
            for q in range(TPB):
                for part in slot_parts(LEAD - 1, q, ALONE):
                    part()
                if q in (1, 2):
                    split_xn2T(0, 2 * q - 2)
                    split_xn2T(0, 2 * q - 1)
            for f in range(AHEAD):
                split_hi(f, f, 0)

            with loop(act, 0, BLOCKS - LEAD) as s:
                ffn_block(s)
            ffn_block(BLOCKS - LEAD, att=False, closing=True)
            with loop(act, BLOCKS - LEAD + 1, BLOCKS - 1) as s:
                ffn_block(s, att=False)
            ffn_block(BLOCKS - 1, att=False, last=True)

        @block.vector
        def _(dve):
            V = nc.vector

            def ln_stats(n, w, src):
                V.bn_stats(stats[w][:], src).then_inc(st_done[w], 1)

            def ln_aggregate(w, last):
                agg = V.bn_aggr(mean_var[:, w, :], stats[w][:])
                if last:
                    agg.then_inc(mv_done, 1)

            def ln_rstd(r):
                wait(dve, ysq_done, r)
                V.scalar_tensor_tensor(out=newton[:], in0=mean_var[:, :, 1], scalar=EPS, in1=y_sq[:],
                                       op0=ALU.add, op1=ALU.mult).then_inc(newton_done, 1)
                wait(dve, newton_done, r)
                V.scalar_tensor_tensor(out=neg_rstd[:], in0=newton[:], scalar=S_NEWTON, in1=y_k[:],
                                       op0=ALU.subtract, op1=ALU.mult).then_inc(rstd_done, 1)
                wait(dve, rstd_done, r)

            def ln_apply(w, src, dst, done):
                V.tensor_scalar(dst, src, mean_var[:, w, 0:1], neg_rstd[:, w:w + 1], ALU.subtract, ALU.mult).then_inc(done, 1)

            def output(n, q, bk):
                wait(dve, coef_done, n)
                wait(dve, o_mm, n)
                V.scalar_tensor_tensor(out=x_ring[:, q, :], in0=bk["o"][:], scalar=coef[:], in1=x_ring[:, q, :],
                                       op0=ALU.mult, op1=ALU.add).then_inc(x2_done, 1)
                wait(dve, x2_done, n)
                ln_stats(n, 1, x_ring[:, q, :])

            def slot_parts(m, q, bk, last_tile=False):
                first = type(m) is int and m == 0 and q == 0
                n = held(dve, 4 * m + q + 1)
                b = sequence_of(dve, m)
                keys = at(b * KEYS, KEYS)
                next_q, prev_q = (q + 1) % 4, (q + 3) % 4

                def part0():
                    if not last_tile:
                        wait(dve, x_loaded[next_q], held(dve, 16 * (m + 1) if q < 3 else 16 * (m + 2)))
                        ln_stats(held(dve, n + 1), 0, x_ring[:, next_q, :])
                    if q > 1:
                        token_sums(held(dve, n - 2), q - 2, m)
                    elif not (type(m) is int and m == 0):
                        token_sums(held(dve, n - 2), q + 2, m - 1)
                    if q == 1 and not (type(m) is int and m == 0):
                        sum_sequence(m)
                    if not first:
                        output(held(dve, n - 1), prev_q, bk)

                def part1():
                    if not first:
                        wait(dve, st_done[1], held(dve, n - 1))
                    if not last_tile:
                        wait(dve, st_done[0], held(dve, n + 1))
                    if q == 0:
                        wait(dve, cb_done, held(dve, b + 1))
                    wait(dve, p_done, held(dve, n - 1))
                    wait(dve, s_mm, n)
                    V.scalar_tensor_tensor(out=neg_s[:], in0=bk["s"][:, 0:KEYS], scalar=-1.0, in1=cb_all[:, keys],
                                           op0=ALU.mult, op1=ALU.subtract).then_inc(negs_done, 1)
                    if not first:
                        ln_aggregate(1, last_tile)
                    if not last_tile:
                        ln_aggregate(0, True)
                    wait(dve, negs_done, n)
                    V.tensor_reduce(neg_max[:], neg_s[:], AX_X, ALU.min).then_inc(s_read, 1)

                def part2():
                    ln_rstd(held(dve, n + 1))
                    if not first:
                        wait(dve, xn2T_mm, held(dve, n - 2))
                        ln_apply(1, x_ring[:, prev_q, :], xn2[:], xn2_done)
                    if not last_tile:
                        wait(dve, xnT_mm, n)
                        ln_apply(0, x_ring[:, next_q, :], xn[:], xn_done)
                    wait(dve, p_done, n)
                    V.reciprocal(p_inv[:], p_sum[:]).then_inc(pinv_done, 1)
                    wait(dve, pinv_done, n)
                    V.tensor_scalar(coef[:], p_inv[:], gate_x[:], NORM, ALU.mult, ALU.mult).then_inc(coef_done, 1)
                    if q == 1 and not (type(m) is int and m == 0):
                        choose_expert(m)

                def part3():
                    pass
                return part0, part1, part2, part3

            def add_bk(b):
                wait(dve, k_mm, held(dve, b + 1))
                V.tensor_tensor(kT, bank[1][:].rearrange("p (k n) -> p k n", k=KD),
                                bk_sb[:].rearrange("p (k o) -> p k o", o=1).to_broadcast([P, KD, P]), ALU.add).then_inc(k_done, 1)

            def add_bv(b):
                wait(dve, v_mm, held(dve, b + 1))
                V.tensor_tensor(v_all[:, at(b, 1), :].rearrange("p o n -> p (o n)"), bank[0][:], bv_sb, ALU.add).then_inc(v_done, 1)

            def token_sums(n, q, m):
                wait(dve, xn2T_done, n)
                in_seq = m % BPS if type(m) is int else nc.s_assert_within(dve.snap(m & (BPS - 1)), 0, BPS - 1, skip_runtime_bounds_check_because="the loop ends at a fixed block")
                col = at(in_seq * TPB + q, 1)
                V.reduce_sum(tok_sums[:, :, col], xn2T_st[:, q % 2], AX_X).then_inc(sum_done, 1)

            def sum_sequence(m):
                wait(dve, sum_done, held(dve, 4 * m))
                V.reduce_sum(xsum[:], tok_sums[:], AX_X).then_inc(xsum_done, 1)

            def choose_expert(m):
                mv = held(dve, m)
                wait(dve, router_mm, mv)
                V.scalar_tensor_tensor(out=logits[:], in0=router_bank[0:1, 0:EXPERTS], scalar=1.0 / SEQ, in1=br_sb[:],
                                       op0=ALU.mult, op1=ALU.add).then_inc(logits_done, 1)
                wait(dve, logits_done, mv)
                V.reduce_max(top[:], logits[:], AX_X).then_inc(top_done, 1)
                wait(dve, top_done, mv)
                V.scalar_tensor_tensor(out=reach[:], in0=logits[:], scalar=top[:], in1=rank_down[:],
                                       op0=ALU.is_ge, op1=ALU.mult).then_inc(reach_done, 1)
                wait(dve, reach_done, mv)
                V.reduce_max(best_rank[:], reach[:], AX_X).then_inc(rank_done, 1)
                wait(dve, rank_done, mv)
                V.tensor_scalar(expert[:, at(m, 1)], best_rank[:], -1.0, float(EXPERTS), ALU.mult, ALU.add).then_inc(expert_done, 1)

            def hidden_lo(c, f):
                wait(dve, h_bank_free, held(dve, c + 3))
                V.tensor_tensor(h_lo[:, f % 2, :], h_full[:, f % 2, :], h_hi[:, f % 2, :].bitcast(F32),
                                ALU.subtract).then_inc(h_lo_done, 1)

            def split_xn2T(s, k):
                wait(dve, xhi_done, held(dve, KD * s + k + 1))
                par = parity(dve, s)
                V.tensor_tensor(xn2T_lo[:, par, k, :].rearrange("p o (t n) -> p (o t) n", n=P), xn2T_raw[:, :, k, :],
                                xn2T_hi[:, par, k, :].rearrange("p o (t n) -> p (o t) n", n=P).bitcast(F32),
                                ALU.subtract).then_inc(xlo_done, 1)

            def add_b2(s, t):
                if t == 0:
                    wait(dve, x2_loaded, held(dve, 16 * s + 16))
                    wait(dve, b2_loaded, held(dve, 16 * (s // BPS + 1) if type(s) is int else 16 * ((s >> 2) + 1)))
                V.scalar_tensor_tensor(out=x2_blk[:, t, :], in0=b2_cur[:], scalar=gate_f[:], in1=x2_blk[:, t, :],
                                       op0=ALU.mult, op1=ALU.add).then_inc(b2_added, 1)

            def finish(s, t):
                if t < TPB - 1:
                    wait(dve, out_mm, held(dve, (TPB - 1) * s + t + 1))
                else:
                    wait(dve, w_slot_free, held(dve, RING + FC * s + FC))
                V.scalar_tensor_tensor(out=x2_blk[:, t, :], in0=out_bank[t][:], scalar=gate_f[:], in1=x2_blk[:, t, :],
                                       op0=ALU.mult, op1=ALU.add).then_inc(out_bank_free, 1)

            def ffn_block(s, att=True, last_att=False, last=False, closing=False):
                for f in range(FC):
                    c = FC * s + f
                    if att and f % 4 == 0:
                        parts = slot_parts(s + LEAD, f // 4, BESIDE, last_att and f == 12)
                    hidden_lo(c, f)
                    if att:
                        parts[f % 4]()
                    if closing and f == 0:
                        output(TILES, 3, BESIDE)
                    if closing and f == 1:
                        wait(dve, st_done[1], TILES)
                        token_sums(TILES - 1, 2, BLOCKS - 1)
                        ln_aggregate(1, True)
                    if closing and f == 3:
                        wait(dve, xn2T_mm, TILES - 1)
                        ln_rstd(TILES + 2)
                        ln_apply(1, x_ring[:, 3, :], xn2[:], xn2_done)
                    if closing and f == 5:
                        token_sums(TILES, 3, BLOCKS - 1)
                        sum_sequence(BLOCKS)
                    if closing and f == 6:
                        choose_expert(BLOCKS)
                    if not last and f >= 8 and f % 2 == 0:
                        split_xn2T(s + 1, (f - 8) // 2)
                    if f >= 8 and f % 2 == 1:
                        add_b2(s, (f - 9) // 2)
                wait(dve, b2_added, held(dve, TPB * s + TPB))
                for t in range(TPB):
                    finish(s, t)

            V.memset(eps_c[:], EPS).then_inc(consts_done, 1)
            V.memset(lnk_c[:], LN_K).then_inc(consts_done, 1)
            V.memset(tok_sums[:], 0.0)
            V.memset(mean_var[:], 1.0).then_inc(consts_done, 1)
            dve.wait_ge(consts_done, 3)
            dve.wait_ge(x_loaded[0], 16)
            ln_stats(1, 0, x_ring[:, 0, :])
            dve.wait_ge(st_done[0], 1)
            ln_aggregate(0, True)
            dve.wait_ge(small_in, 16 * 8)
            add_bk(0)
            V.tensor_copy(bqb, bq_sb[:].rearrange("p (k o) -> p k o", o=1).to_broadcast([P, KD, P])).then_inc(consts_done, 1)
            for h in (1, 3):
                dve.wait_ge(wqT_mm, h + 1)
                V.tensor_copy(wqT[:, h, :], bank[3 + h][:]).then_inc(wqT_dve, 1)
            dve.wait_ge(gates_done, 1)
            V.tensor_copy(gate_x[:], gates[:, 0:1])
            V.tensor_copy(gate_f[:], gates[:, 1:2]).then_inc(consts_done, 1)
            ln_rstd(1)
            ln_apply(0, x_ring[:, 0, :], xn[:], xn_done)
            add_bv(0)
            dve.wait_ge(consts_done, 5)

            for q in range(TPB):
                for part in slot_parts(0, q, ALONE):
                    part()
            with loop(dve, 1, BATCH) as m:
                for q in range(TPB):
                    if q == 2:
                        add_bk(m)
                    if q == 3:
                        add_bv(m)
                    for part in slot_parts(m, q, ALONE):
                        part()
            for q in range(TPB):
                for part in slot_parts(LEAD - 1, q, ALONE):
                    part()
                if q in (2, 3):
                    split_xn2T(0, 2 * q - 4)
                    split_xn2T(0, 2 * q - 3)

            with loop(dve, 0, BLOCKS - LEAD - 1) as s:
                ffn_block(s)
            ffn_block(BLOCKS - LEAD - 1, last_att=True)
            ffn_block(BLOCKS - LEAD, att=False, closing=True)
            with loop(dve, BLOCKS - LEAD + 1, BLOCKS - 1) as s:
                ffn_block(s, att=False)
            ffn_block(BLOCKS - 1, att=False, last=True)

        @block.gpsimd
        def _(pool):
            with loop(pool, 0, BLOCKS) as s:
                for f in range(FC):
                    wait(pool, w_hi_done, held(pool, FC * s + f + 1))
                    nc.gpsimd.tensor_tensor(w_lo[:, f % RING, :], w_raw[:, f, 0:2 * D],
                                            w_hi[:, f % RING, :].bitcast(F32), ALU.subtract)
                    nc.gpsimd.tensor_copy(b1_cur[:, f:f + 1], w_raw[:, f, 2 * D:2 * D + 1]).then_inc(w_lo_done, 1)


LN_K = -0.23104906018664842

_INS = ["x", "ctx_1024", "g_xattn", "g_ffn", "L0_xattn_Wq", "L0_xattn_bq", "L0_xattn_Wk", "L0_xattn_bk",
        "L0_xattn_Wv", "L0_xattn_bv", "L0_ffn_Wr", "L0_ffn_br", "L0_ffn_W1", "L0_ffn_b1", "L0_ffn_W2", "L0_ffn_b2"]


def kernel(**inputs):
    import numpy as np
    import concourse.bacc as bacc
    from concourse.bass_utils import run_bass_kernel_spmd

    nc = bacc.Bacc("TRN2", target_bir_lowering=False, num_devices=1)
    arrays, args = {}, []
    for name in _INS:
        a = np.ascontiguousarray(inputs[name])
        if name == "x":
            a = a.reshape(BLOCKS, TPB, P, D)
        arrays[f"in_{name}"] = a
        args.append(nc.dram_tensor(f"in_{name}", a.shape, mybir.dt.from_np(a.dtype), kind="ExternalInput").ap())
    arrays["identity"] = np.eye(P, dtype=np.float32)
    args.append(nc.dram_tensor("identity", (P, P), F32, kind="ExternalInput").ap())
    arrays["rank_down"] = np.arange(EXPERTS, 0, -1, dtype=np.float32)[None, :]
    args.append(nc.dram_tensor("rank_down", (1, EXPERTS), F32, kind="ExternalInput").ap())
    out = nc.dram_tensor("out", (BLOCKS, TPB, P, D), F32, kind="ExternalOutput").ap()
    gated_block(nc, *args, out.rearrange("s t p n -> s p t n"))
    got = run_bass_kernel_spmd(nc, [arrays], core_ids=[0])
    return got.results[0]["out"].reshape(BATCH, SEQ, D)
```

```python
from contextlib import ExitStack
from math import log

import concourse.bass as bass
from concourse import mybir

F32 = mybir.dt.float32
F32R = mybir.dt.float32r
U32 = mybir.dt.uint32
ALU = mybir.AluOpType
ACT = mybir.ActivationFunctionType
AX_X = mybir.AxisListType.X

P = 128
BATCH, SEQ, D = 4, 2048, 512
KEYS = 128
HIDDEN = 2048
EXPERTS = 8
KD = D // P
B32 = 32
NB = P // B32
ROWS = 512
TPB = ROWS // P
BLOCKS = BATCH * SEQ // ROWS
BPS = SEQ // ROWS
TILES = BLOCKS * TPB
FC = HIDDEN // P
LEAD = BPS + 1
RING = 4
AHEAD = 3
EPS = 1e-5
NORM = float(D) ** -0.5
K_NEWTON = 0.5 ** (1.0 / 3.0)
S_NEWTON = 3.0 * K_NEWTON * K_NEWTON
LN_K = log(K_NEWTON)


def gated_block(nc, x, ctx_in, g_xattn, g_ffn, wq, bq, wk, bk, wv, bv, wr, br, w1, b1, w2, b2, ident_in, rank_in, out):
    ctx = ExitStack()
    with ctx:
        def sb(name, shape, dt=F32):
            return ctx.enter_context(nc.sbuf_tensor(name, shape, dt))

        def sem(name):
            return ctx.enter_context(nc.semaphore(name))

        x2_dram = nc.dram_tensor("x2_dram", (TILES, P, D), F32, kind="Internal").ap()
        xnT_dram = nc.dram_tensor("xnT_dram", (2, B32, NB, KD, NB, B32), F32, kind="Internal").ap()
        xn2T_dram = nc.dram_tensor("xn2T_dram", (TILES, P, D), F32, kind="Internal").ap()

        w_raw = sb("w_raw", [P, FC, 2 * D + 1])
        w_hi = sb("w_hi", [P, RING, 2 * D], F32R)
        w_lo = sb("w_lo", [P, RING, 2 * D], F32R)
        b1_cur = sb("b1_cur", [P, FC])
        b2_cur = sb("b2_cur", [P, D])
        xn2T_raw = sb("xn2T_raw", [P, TPB * NB, KD, B32])
        xn2T_hi = sb("xn2T_hi", [P, 2, KD, ROWS], F32R)
        xn2T_lo = sb("xn2T_lo", [P, 2, KD, ROWS], F32R)
        x2_blk = sb("x2_blk", [P, TPB, D])
        h_full = sb("h_full", [P, 2, ROWS])
        h_hi = sb("h_hi", [P, 2, ROWS], F32R)
        h_lo = sb("h_lo", [P, 2, ROWS], F32R)
        m_all = sb("m_all", [P, KD, BATCH * KEYS])
        v_all = sb("v_all", [P, BATCH, D])
        cb_all = sb("cb_all", [P, BATCH * KEYS])
        ident = sb("ident", [P, P])
        wr_sb = sb("wr_sb", [P, KD, NB, EXPERTS])
        ones = sb("ones", [P, 1])
        br_sb = sb("br_sb", [1, EXPERTS])
        gates = sb("gates", [P, 2])
        gate_x = sb("gate_x", [P, 1])
        gate_f = sb("gate_f", [P, 1])
        eps_c = sb("eps_c", [P, 1])
        lnk_c = sb("lnk_c", [P, 1])
        bk_sb = sb("bk_sb", [P, KD])
        bq_sb = sb("bq_sb", [P, KD])
        x_ring = sb("x_ring", [P, 4, D])
        xn = sb("xn", [P, D])
        xnT = sb("xnT", [P, KD, P])
        xnT_st = sb("xnT_st", [P, NB, KD, B32])
        neg_s = sb("neg_s", [P, KEYS])
        neg_max = sb("neg_max", [P, 1])
        probs = sb("probs", [P, KEYS])
        p_sum = sb("p_sum", [P, 1])
        p_inv = sb("p_inv", [P, 1])
        coef = sb("coef", [P, 1])
        pT = sb("pT", [P, P])
        xn2 = sb("xn2", [P, D])
        xn2T_st = sb("xn2T_st", [P, 2, NB, KD, B32])
        tile_sum = sb("tile_sum", [P, D])
        blk_sums = sb("blk_sums", [P, NB, KD, BPS])
        stats = [sb(f"stats{n}", [P, 6]) for n in (1, 2)]
        mean_var = sb("mean_var", [P, 2, 2])
        ln_v, y_k, y_sq, newton, neg_rstd = (sb(n, [P, 2]) for n in ("ln_v", "y_k", "y_sq", "newton", "neg_rstd"))
        seq_sums = sb("seq_sums", [P, NB, KD])
        weighted = sb("weighted", [P, EXPERTS, NB * KD])
        score_parts = sb("score_parts", [P, EXPERTS])
        logits = sb("logits", [1, EXPERTS])
        rank_down = sb("rank_down_sb", [1, EXPERTS])
        top = sb("top", [1, 1])
        reach = sb("reach", [1, EXPERTS])
        best_rank = sb("best_rank", [1, 1])
        expert = sb("expert", [1, BLOCKS + 1], U32)

        def in_w(at, n):
            per = (2 * D + 1) * FC
            flat = w_raw[:].rearrange("p f n -> p (f n)")
            assert (at + 1) * KD * D <= per
            return flat[:, at * KD * D:at * KD * D + KD * n].rearrange("p (k n) -> p k n", k=KD)

        wk_sb, wq_sb, wv_sb, wqT = (in_w(i, D) for i in range(4))
        bqb, ctxT, kT = in_w(4, P), in_w(5, P), in_w(6, P)
        ctx_seq = in_w(7, P).rearrange("p k n -> p (k n)")
        bv_sb = x2_blk[:, 0, :]

        bank = [ctx.enter_context(nc.psum_tensor(f"bank{i}", [P, 512], F32)) for i in range(8)]
        out_bank = bank[0:4]
        h_bank = bank[4:6]
        BESIDE = dict(s=bank[6], pT=bank[6], o=bank[6], router=bank[7])
        ALONE = dict(s=bank[6], pT=bank[5], o=bank[4], xnT=bank[7], router=bank[5])

        ident_in_sem, wq_in, wv_in, small_in = (sem(n) for n in ("ident_in", "wq_in", "wv_in", "small_in"))
        bk_in, bq_in, router_in = sem("bk_in"), sem("bq_in"), sem("router_in")
        wk_in = [sem(f"wk_in{half}") for half in range(2)]
        wqT_mm, wqT_act, wqT_dve, consts_done = (sem(n) for n in ("wqT_mm", "wqT_act", "wqT_dve", "consts_done"))
        ctx_loaded, ctxT_mm, ctxT_done = sem("ctx_loaded"), sem("ctxT_mm"), sem("ctxT_done")
        k_mm, k_done, m_mm, m_done = (sem(n) for n in ("k_mm", "k_done", "m_mm", "m_done"))
        v_mm, v_done, cb_mm, cb_done = (sem(n) for n in ("v_mm", "v_done", "cb_mm", "cb_done"))
        gates_done, warm_done = sem("gates_done"), sem("warm_done")
        x_loaded = [sem(f"x_loaded{i}") for i in range(4)]
        x2_stored = [sem(f"x2_stored{i}") for i in range(4)]
        xn2T_stored = [sem(f"xn2T_stored{i}") for i in range(2)]
        st_done = [sem(f"st_done{n}") for n in (1, 2)]
        mv_done, lnv_done, yk_done, ysq_done, newton_done, rstd_done = (
            sem(n) for n in ("mv_done", "lnv_done", "yk_done", "ysq_done", "newton_done", "rstd_done"))
        xnT_st_done, xnT_stored, xnT_ready = sem("xnT_st_done"), sem("xnT_stored"), sem("xnT_ready")
        xn_done, xnT_mm, xnT_done = sem("xn_done"), sem("xnT_mm"), sem("xnT_done")
        s_mm, negs_done, s_read, p_done = (sem(n) for n in ("s_mm", "negs_done", "s_read", "p_done"))
        pT_mm, pT_done = sem("pT_mm"), sem("pT_done")
        pinv_done, coef_done, o_mm, x2_done = (sem(n) for n in ("pinv_done", "coef_done", "o_mm", "x2_done"))
        xn2_done, xn2T_done = sem("xn2_done"), sem("xn2T_done")
        tiles_summed = sem("tiles_summed")
        blk_done, seq_done, weighted_done, parts_done, router_mm, logits_done, top_done, reach_done, rank_done, expert_done = (
            sem(n) for n in ("blk_done", "seq_done", "weighted_done", "parts_done", "router_mm", "logits_done", "top_done", "reach_done", "rank_done", "expert_done"))
        w_loaded = [sem(f"w_loaded{f}") for f in range(FC)]
        b2_loaded = sem("b2_loaded")
        w_hi_done, w_lo_done, w_slot_free = sem("w_hi_done"), sem("w_lo_done"), sem("w_slot_free")
        xn2T_loaded, x2_loaded, out_stored = sem("xn2T_loaded"), sem("x2_loaded"), sem("out_stored")
        xhi_done, xlo_done = sem("xhi_done"), sem("xlo_done")
        h_mm, h_bank_free, h_hi_done, h_lo_done = (sem(n) for n in ("h_mm", "h_bank_free", "h_hi_done", "h_lo_done"))
        b2_added, out_mm, out_bank_free = sem("b2_added"), sem("out_mm"), sem("out_bank_free")

        def rows_of(w):
            return w.rearrange("(k p) n -> p k n", p=P)

        def loop(eng, lo, hi):
            return nc.Fori(lo, hi, engines=[eng.engine], hint_back_edge=True)

        def held(eng, v):
            return v if type(v) is int else eng.snap(eng.to_reg(v) if eng.engine == mybir.EngineType.SP else v)

        def wait(eng, s, v):
            if type(v) is not int or v > 0:
                eng.wait_ge(s, v)

        def sequence_of(eng, blk):
            return blk // BPS if type(blk) is int else nc.s_assert_within(eng.snap(blk >> 2), 0, BATCH - 1, skip_runtime_bounds_check_because="the loop ends at a fixed block")

        def parity(eng, blk):
            return at(blk % 2 if type(blk) is int else nc.s_assert_within(eng.snap(blk & 1), 0, 1, skip_runtime_bounds_check_because="the loop ends at a fixed block"), 1)

        def at(start, size):
            return slice(start, start + size) if type(start) is int else bass.ds(start, size)

        block = ctx.enter_context(nc.Block())

        @block.sync
        def _(sp):
            x2_blocks = x2_dram.rearrange("(s t) p n -> s p t n", t=TPB)
            xn2T_blocks = xn2T_dram.rearrange("(s t) (i r) (a kc) -> s a r (t i) kc", t=TPB, r=B32, a=NB)

            def load_x(m, q):
                sp.dma_start(x_ring[:, q, :], x[m, q]).then_inc(x_loaded[q], 16)

            def store_x2(m, q):
                n = held(sp, 4 * m + q + 1)
                wait(sp, x2_done, n)
                sp.dma_start(x2_dram[n - 1], x_ring[:, q, :]).then_inc(x2_stored[q], 16)

            def store_xn2T(m, q):
                n = held(sp, 4 * m + q + 1)
                wait(sp, xn2T_done, n)
                sp.dma_start(xn2T_dram[n - 1], xn2T_st[:, q % 2]).then_inc(xn2T_stored[q % 2], 16)

            def stores(m, q):
                first = type(m) is int and m == 0
                if q > 0:
                    store_x2(m, q - 1)
                elif not first:
                    store_x2(m - 1, 3)
                if q > 1:
                    store_xn2T(m, q - 2)
                elif not first:
                    store_xn2T(m - 1, q + 2)

            def load_ahead(m, q, last=False):
                if type(m) is int and m == 0 and q == 0:
                    load_x(m, 3)
                elif q == 0 or not last:
                    stored, normed = held(sp, 16 * (m + 1) if q else 16 * m), held(sp, 4 * m + q)
                    wait(sp, x2_stored[(q + 3) % 4], stored)
                    wait(sp, xn2_done, normed)
                    if q == 0:
                        load_x(m, 3)
                    else:
                        load_x(m + 1, q - 1)

            def turn_xn(n, q):
                turn, stored, used = (held(sp, v) for v in (n - (LEAD * TPB - 1), 16 * NB * (n - (LEAD * TPB - 1)), n))
                wait(sp, xnT_st_done, turn)
                for i in range(NB):
                    sp.dma_start(xnT_dram[q % 2][:, :, :, i, :].rearrange("r a k c -> r (a k) c"),
                                 xnT_st[i * B32:(i + 1) * B32].rearrange("p a k c -> p (a k) c")).then_inc(xnT_stored, 16)
                wait(sp, xnT_stored, stored)
                wait(sp, s_mm, used)
                sp.dma_start(xnT[:].rearrange("p k n -> p (k n)"),
                             xnT_dram[q % 2].rearrange("r a k i c -> a r (k i c)")).then_inc(xnT_ready, 16)

            def load_ctx(b):
                wait(sp, ctxT_mm, held(sp, b))
                sp.dma_start(ctx_seq, ctx_in[b]).then_inc(ctx_loaded, 16)

            def load_chunks(e, f0, f1, used):
                for f in range(f0, f1):
                    if used is not None:
                        wait(sp, w_lo_done, held(sp, used + f + 1))
                    cols = slice(f * P, (f + 1) * P)
                    sp.dma_start(w_raw[:, f, 0:D].rearrange("p (k n) -> p k n", k=KD),
                                 w1[bass.ds(e, 1), :, cols].rearrange("e (k p) n -> p (e k) n", p=P)).then_inc(w_loaded[f], 16)
                    sp.dma_start(w_raw[:, f, D:2 * D], w2[bass.ds(e, 1), cols, :].rearrange("e p n -> p (e n)")).then_inc(w_loaded[f], 16)
                    with nc.allow_non_contiguous_dma(reason="one bias per partition"):
                        sp.dma_start(w_raw[:, f, 2 * D:2 * D + 1],
                                     b1[bass.ds(e, 1), cols].rearrange("e p -> p e")).then_inc(w_loaded[f], 16)

            def load_b2(e, used):
                if used is not None:
                    wait(sp, b2_added, held(sp, used))
                sp.dma_start(b2_cur[:], b2[bass.ds(e, 1), :].rearrange("e n -> (e n)").partition_broadcast(P)).then_inc(b2_loaded, 16)

            def chosen(m):
                wait(sp, expert_done, held(sp, m - (BPS - 1)))
                return sp.value_load(expert[0:1, m:m + 1], min_val=0, max_val=EXPERTS - 1)

            def load_xn2T(s):
                stored, split = held(sp, 32 * s + 32), held(sp, KD * s)
                for par in range(2):
                    wait(sp, xn2T_stored[par], stored)
                wait(sp, xhi_done, split)
                wait(sp, xlo_done, split)
                for a in range(NB):
                    sp.dma_start(xn2T_raw[a * B32:(a + 1) * B32].rearrange("p t k c -> p t (k c)"),
                                 xn2T_blocks[s, a]).then_inc(xn2T_loaded, 16)

            def store_out(s):
                wait(sp, out_bank_free, held(sp, 4 * s + 8))
                sp.dma_start(out[s], x2_blk[:]).then_inc(out_stored, 16)

            def load_x2(s):
                stored, free = held(sp, 16 * s + 16), held(sp, 16 * s)
                for q in range(TPB):
                    wait(sp, x2_stored[q], stored)
                wait(sp, out_stored, free)
                sp.dma_start(x2_blk[:], x2_blocks[s]).then_inc(x2_loaded, 16)

            def ffn_block(s, att=True, last_att=False, switch=False, closing=False, e=None):
                m = s + LEAD
                if att:
                    stores(m, 0)
                if closing:
                    store_x2(BLOCKS - 1, 3)
                    store_xn2T(BLOCKS - 1, 2)
                if not (type(s) is int and s == 0):
                    store_out(s - 1)
                if type(s) is not int or s < BLOCKS - 1:
                    load_xn2T(s + 1)
                load_x2(s)
                if closing:
                    store_xn2T(BLOCKS - 1, 3)
                    e = chosen(m)
                    load_chunks(e, 0, FC, FC * s)
                    load_b2(e, 4 * s + 4)
                for q in range(TPB) if att else []:
                    if q > 0:
                        stores(m, q)
                    load_ahead(m, q, last_att)
                    if not (last_att and q == TPB - 1):
                        turn_xn(4 * m + q + 1, (q + 1) % 4)
                    if e is not None and q == 0:
                        load_chunks(e, 10, 13, FC * (s - 1) if s > 0 else None)
                        load_b2(e, 4 * s if s > 0 else None)
                    if e is not None and q == 1:
                        load_chunks(e, 13, FC, FC * (s - 1) if s > 0 else None)
                    if switch and q == 2:
                        e_next = chosen(m)
                        load_chunks(e_next, 0, 4, FC * s)
                    if switch and q == 3:
                        load_chunks(e_next, 4, 10, FC * s)
                return e_next if switch else None

            sp.dma_start(ident[:], ident_in).then_inc(ident_in_sem, 16)
            load_ctx(0)
            for half in range(2):
                cols = slice(half * D // 2, (half + 1) * D // 2)
                sp.dma_start(wk_sb[:, :, cols], rows_of(wk)[:, :, cols]).then_inc(wk_in[half], 16)
            load_x(0, 0)
            with nc.allow_non_contiguous_dma(reason="small vectors, one value per partition"):
                sp.dma_start(bk_sb[:], bk.rearrange("(k p) -> p k", p=P)).then_inc(bk_in, 16)
                sp.dma_start(wq_sb, rows_of(wq)).then_inc(wq_in, 16)
                sp.dma_start(bq_sb[:], bq.rearrange("(k p) -> p k", p=P)).then_inc(bq_in, 16)
            sp.dma_start(gates[:, 0:1], g_xattn.partition_broadcast(P)).then_inc(small_in, 16)
            sp.dma_start(gates[:, 1:2], g_ffn.partition_broadcast(P)).then_inc(small_in, 16)
            sp.dma_start(wv_sb, rows_of(wv)).then_inc(wv_in, 16)
            load_x(0, 1)
            sp.dma_start(bv_sb, bv.partition_broadcast(P)).then_inc(small_in, 16)
            for i in range(NB):
                sp.dma_start(wr_sb[i * B32:(i + 1) * B32].rearrange("p k a e -> p (k a) e"),
                             wr.rearrange("(g r) e -> r g e", r=B32)).then_inc(router_in, 16)
            sp.dma_start(br_sb[:], br[None, :]).then_inc(router_in, 16)
            sp.dma_start(rank_down[:], rank_in).then_inc(router_in, 16)
            load_x(0, 2)
            load_ctx(1)

            for q in range(TPB):
                stores(0, q)
                load_ahead(0, q)
            with loop(sp, 1, BATCH - 1) as m:
                load_ctx(m + 1)
                for q in range(TPB):
                    stores(m, q)
                    load_ahead(m, q)
            load_xn2T(0)
            for q in range(TPB):
                stores(BATCH - 1, q)
                load_ahead(BATCH - 1, q)
            stores(LEAD - 1, 0)
            load_ahead(LEAD - 1, 0)
            stores(LEAD - 1, 1)
            load_ahead(LEAD - 1, 1)
            e = chosen(LEAD - 1)
            load_chunks(e, 0, 3, None)
            stores(LEAD - 1, 2)
            load_ahead(LEAD - 1, 2)
            load_chunks(e, 3, 6, None)
            stores(LEAD - 1, 3)
            load_ahead(LEAD - 1, 3)
            sp.sem_inc(xnT_stored, 16 * NB)
            load_chunks(e, 6, 10, None)

            ffn_block(0, e=e)
            with loop(sp, 1, 3) as s:
                ffn_block(s)
            e = ffn_block(3, switch=True)
            ffn_block(4, e=e)
            with loop(sp, 5, 7) as s:
                ffn_block(s)
            e = ffn_block(7, switch=True)
            ffn_block(8, e=e)
            ffn_block(9)
            ffn_block(10, last_att=True)
            ffn_block(11, att=False, closing=True)
            with loop(sp, 12, 15) as s:
                ffn_block(s, att=False)
            ffn_block(15, att=False)
            for t in range(TPB):
                sp.wait_ge(out_bank_free, TPB * BLOCKS + t + 1)
                sp.dma_start(out[BLOCKS - 1][:, t, :], x2_blk[:, t, :]).then_inc(out_stored, 16)
            sp.wait_ge(out_stored, 16 * (BLOCKS - 1 + TPB))
            for q in range(4):
                sp.wait_ge(x2_stored[q], 16 * BLOCKS)
            for par in range(2):
                sp.wait_ge(xn2T_stored[par], 32 * BLOCKS)

        @block.tensor
        def _(pe):
            def mm(dst, lhsT, rhs, start, stop):
                return pe.matmul(dst, lhsT, rhs, start=start, stop=stop)

            def transpose_xn(n, bk):
                wait(pe, xn_done, n)
                for k in range(KD):
                    last = pe.transpose(bk["xnT"][:, k * P:(k + 1) * P], xn[:, k * P:(k + 1) * P], ident[:])
                last.then_inc(xnT_mm, 1)

            def scores(n, bk, b, q):
                if bk is ALONE:
                    wait(pe, xnT_done, n)
                else:
                    wait(pe, xnT_ready, held(pe, 16 * (n - LEAD * TPB)))
                if bk is BESIDE:
                    wait(pe, x2_done, held(pe, n - 1))
                if q == 0:
                    wait(pe, m_done, held(pe, b + 1))
                for k in range(KD):
                    last = mm(bk["s"][:, 0:KEYS], xnT[:, k, :], m_all[:, k, at(b * KEYS, KEYS)], k == 0, k == KD - 1)
                last.then_inc(s_mm, 1)

            def transpose_p(n, bk, q, m):
                wait(pe, p_done, n)
                if bk is ALONE and q == 2 and type(m) is int and m == LEAD - 1:
                    wait(pe, logits_done, 1)
                pe.transpose(bk["pT"][:, 0:P], probs[:], ident[:]).then_inc(pT_mm, 1)

            def attend(n, bk, b, q):
                wait(pe, pT_done, n)
                if bk is ALONE:
                    wait(pe, x2_done, held(pe, n - 1))
                if q == 0:
                    wait(pe, v_done, held(pe, b + 1))
                mm(bk["o"][:], pT[:], v_all[:, at(b, 1), :].rearrange("p o n -> p (o n)"), True, True).then_inc(o_mm, 1)

            def router(m, bk):
                turn = m - (BPS - 1)
                wait(pe, logits_done, turn - 1 if type(turn) is int else held(pe, turn - 1))
                wait(pe, parts_done, held(pe, turn))
                mm(bk["router"][0:1, 0:EXPERTS], ones[:], score_parts[:], True, True).then_inc(router_mm, 1)

            def slot_parts(m, q, bk):
                o_bk = BESIDE if type(m) is int and m == LEAD - 1 and q == TPB - 1 else bk
                n = held(pe, 4 * m + q + 1)
                b = sequence_of(pe, m)

                def part1():
                    scores(n, bk, b, q)

                def part2():
                    transpose_p(n, bk, q, m)
                    if bk is BESIDE and q == 2:
                        router(m, bk)

                def part3():
                    attend(n, o_bk, b, q)
                return part1, part2, part3

            def ctx_transpose(b):
                wait(pe, ctx_loaded, held(pe, 16 * b + 16))
                wait(pe, v_done, held(pe, b))
                for k in range(KD):
                    last = pe.transpose(bank[0][:, k * P:(k + 1) * P], ctx_seq[:, k * P:(k + 1) * P], ident[:])
                last.then_inc(ctxT_mm, 1)

            def keys_part(b, h0, h1):
                if h0 == 0:
                    wait(pe, ctxT_done, held(pe, b + 1))
                    wait(pe, cb_done, held(pe, b))
                for h in range(h0, h1):
                    for k in range(KD):
                        last = mm(bank[1][:, h * P:(h + 1) * P], wk_sb[:, k, h * P:(h + 1) * P], ctxT[:, k, :], k == 0, k == KD - 1)
                if h1 == KD:
                    last.then_inc(k_mm, 1)

            def values_part(b, k0, k1):
                for k in range(k0, k1):
                    last = mm(bank[0][:], ctxT[:, k, :], wv_sb[:, k, :], k == 0, k == KD - 1)
                if k1 == KD:
                    last.then_inc(v_mm, 1)

            def folded_part(b, d0, d1):
                if d0 == 0:
                    wait(pe, k_done, held(pe, b + 1))
                    wait(pe, m_done, held(pe, b))
                for d in range(d0, d1):
                    for h in range(KD):
                        last = mm(bank[2][:, d * P:(d + 1) * P], wqT[:, h, d * P:(d + 1) * P], kT[:, h, :], h == 0, h == KD - 1)
                if d1 == KD:
                    last.then_inc(m_mm, 1)

            def bias_scores(b):
                for h in range(KD):
                    last = mm(bank[1][:, 0:KEYS], bqb[:, h, :], kT[:, h, :], h == 0, h == KD - 1)
                last.then_inc(cb_mm, 1)

            def keys_pieces(b, i0, i1):
                for i in range(i0, i1):
                    if i == 0:
                        ctx_transpose(b)
                    elif i <= KD:
                        keys_part(b, i - 1, i)
                    elif i <= 2 * KD:
                        values_part(b, i - KD - 1, i - KD)
                    elif i <= 3 * KD:
                        folded_part(b, i - 2 * KD - 1, i - 2 * KD)
                    else:
                        bias_scores(b)

            def keep_clock():
                for _ in range(2 * KD):
                    mm(bank[3][:, 0:P], ident[:], ident[:], True, True)

            def attention_block(m, beside, keep=()):
                last_block = type(m) is int and m == LEAD - 1
                for q in range(TPB):
                    part1, part2, part3 = slot_parts(m, q, ALONE)
                    part1()
                    if q == 2 and last_block:
                        router(m, ALONE)
                    for b, i0, i1 in beside[q]:
                        keys_pieces(b, i0, i1)
                    if q in keep:
                        keep_clock()
                    part2()
                    transpose_xn(held(pe, 4 * m + q + 2), ALONE)
                    part3()
                    if q == 0 and type(m) is int and m == 0:
                        ctx_transpose(1)

            def ffn_up(c, f, xs):
                wait(pe, w_lo_done, held(pe, c + 1))
                wait(pe, h_bank_free, held(pe, c + 1))
                dst, slot = h_bank[f % 2][:], f % RING
                for k in range(KD):
                    hi = w_hi[:, slot, k * P:(k + 1) * P]
                    lo = w_lo[:, slot, k * P:(k + 1) * P]
                    mm(dst, hi, xn2T_hi[:, xs, k, :].rearrange("p o n -> p (o n)"), k == 0, False)
                    mm(dst, hi, xn2T_lo[:, xs, k, :].rearrange("p o n -> p (o n)"), False, False)
                    last = mm(dst, lo, xn2T_hi[:, xs, k, :].rearrange("p o n -> p (o n)"), False, k == KD - 1)
                last.then_inc(h_mm, 1)

            def ffn_down(c, f):
                slot = f % RING
                whi, wlo = w_hi[:, slot, D:2 * D], w_lo[:, slot, D:2 * D]
                n = held(pe, c + 1)
                wait(pe, h_hi_done, n)
                for t in range(TPB):
                    if f == 0:
                        wait(pe, out_bank_free, held(pe, 4 * (c // FC) + t + 1 if type(c) is int else (c >> 2) + t + 1))
                    cols = slice(t * P, (t + 1) * P)
                    mm(out_bank[t][:], h_hi[:, f % 2, cols], whi, f == 0, False)
                    mm(out_bank[t][:], h_hi[:, f % 2, cols], wlo, False, False)
                wait(pe, h_lo_done, n)
                for t in range(TPB):
                    last = mm(out_bank[t][:], h_lo[:, f % 2, t * P:(t + 1) * P], whi, False, f == FC - 1)
                    if f == FC - 1 and t < TPB - 1:
                        last.then_inc(out_mm, 1)
                last.then_inc(w_slot_free, 1)

            def first_up(s):
                wait(pe, xlo_done, held(pe, KD * s + KD))
                ffn_up(FC * s, 0, parity(pe, s))

            def ffn_block(s, att=True, closing=False, last=False):
                xs = parity(pe, s)
                for f in range(FC):
                    c = FC * s + f
                    if att and f % 4 == 0:
                        parts = slot_parts(s + LEAD, f // 4, BESIDE)
                    if f > 0:
                        ffn_up(c, f, xs)
                        ffn_down(c - 1, f - 1)
                    if att and f % 4 > 0:
                        parts[f % 4 - 1]()
                    if closing and f == 9:
                        router(BLOCKS, BESIDE)
                ffn_down(FC * s + FC - 1, FC - 1)
                if not last:
                    first_up(s + 1)

            def warm_up(n):
                for _ in range(n):
                    mm(bank[7][:, 0:P], probs[:], probs[:], True, True)

            pe.wait_ge(warm_done, 1)
            warm_up(6)

            pe.wait_ge(ident_in_sem, 16)
            ctx_transpose(0)
            warm_up(4)
            for half in range(2):
                pe.wait_ge(wk_in[half], 16)
                keys_part(0, half * KD // 2, (half + 1) * KD // 2)
            pe.wait_ge(wq_in, 16)
            for h in range(KD):
                for k in range(KD):
                    last = pe.transpose(bank[3 + h][:, k * P:(k + 1) * P], wq_sb[:, k, h * P:(h + 1) * P], ident[:])
                last.then_inc(wqT_mm, 1)
            pe.sem_inc(w_slot_free, RING)
            pe.wait_ge(wv_in, 16)
            values_part(0, 0, 2)
            pe.wait_ge(wqT_act, 2)
            pe.wait_ge(wqT_dve, 2)
            folded_part(0, 0, KD)
            transpose_xn(1, ALONE)
            pe.wait_ge(router_in, 16 * (NB + 2))
            pe.wait_ge(consts_done, 4)
            bias_scores(0)
            attention_block(0, [[(0, 7, 9)], [(1, 1, 4)], [(1, 4, 6)], [(1, 6, 7)]], keep=(3,))
            with loop(pe, 1, BATCH - 1) as m:
                attention_block(m, [[(m, 7, 11)], [(m, 11, 14), (m + 1, 0, 1)], [(m + 1, 1, 4)], [(m + 1, 4, 7)]])
            b = BATCH - 1
            attention_block(b, [[(b, 7, 9)], [(b, 9, 11)], [(b, 11, 13)], [(b, 13, 14)]], keep=(3,))
            attention_block(LEAD - 1, [[]] * TPB, keep=range(TPB))
            pe.wait_ge(x2_done, LEAD * TPB - 1)
            pe.sem_inc(h_bank_free, 2)
            first_up(0)

            pe.wait_ge(cb_done, BATCH)
            pe.wait_ge(m_done, BATCH)
            pe.wait_ge(v_done, BATCH)
            pe.sem_inc(out_bank_free, TPB)

            with loop(pe, 0, BLOCKS - LEAD) as s:
                ffn_block(s)
            ffn_block(BLOCKS - LEAD, att=False, closing=True)
            with loop(pe, BLOCKS - LEAD + 1, BLOCKS - 1) as s:
                ffn_block(s, att=False)
            ffn_block(BLOCKS - 1, att=False, last=True)

        @block.scalar
        def _(act):
            A = nc.scalar.activation

            def ln_v_of(r):
                wait(act, mv_done, r)
                A(ln_v[:], mean_var[:, :, 1], ACT.Ln, bias=eps_c[:]).then_inc(lnv_done, 1)

            def inverse_roots(r):
                wait(act, lnv_done, r)
                A(y_k[:], ln_v[:], ACT.Exp, bias=lnk_c[:], scale=-0.5).then_inc(yk_done, 1)
                wait(act, yk_done, r)
                A(y_sq[:], y_k[:], ACT.Square).then_inc(ysq_done, 1)

            def exp_scores(n):
                wait(act, s_read, n)
                A(probs[:], neg_s[:], ACT.Exp, bias=neg_max[:], scale=-1.0, accum_out=p_sum[:]).then_inc(p_done, 1)

            def copy_pT(n, bk):
                wait(act, pT_mm, n)
                wait(act, o_mm, held(act, n - 1))
                A(pT[:], bk["pT"][:, 0:P], ACT.Copy).then_inc(pT_done, 1)

            def copy_xnT(n, bk, done=xnT_done, step=1):
                wait(act, xnT_mm, n)
                wait(act, s_mm, held(act, n - 1))
                A(xnT[:].rearrange("p k n -> p (k n)"), bk["xnT"][:], ACT.Copy).then_inc(done, step)

            def slot_parts(m, q, bk):
                n = held(act, 4 * m + q + 1)

                def part0():
                    if bk is ALONE:
                        copy_xnT(n, bk)

                def part1():
                    r = held(act, n + 1)
                    ln_v_of(r)
                    if bk is BESIDE:
                        exp_scores(n)
                    inverse_roots(r)
                    if bk is ALONE:
                        exp_scores(n)

                def part2():
                    copy_pT(n, bk)
                return part0, part1, part2

            def copy_ctxT(b):
                wait(act, ctxT_mm, held(act, b + 1))
                A(ctxT.rearrange("p k n -> p (k n)"), bank[0][:], ACT.Copy).then_inc(ctxT_done, 1)

            def add_bk(b):
                wait(act, k_mm, held(act, b + 1))
                for h in range(KD):
                    last = A(kT[:, h, :], bank[1][:, h * P:(h + 1) * P], ACT.Identity, bias=bk_sb[:, h:h + 1])
                last.then_inc(k_done, 1)

            def copy_folded(b):
                wait(act, m_mm, held(act, b + 1))
                A(m_all[:, :, at(b * KEYS, KEYS)], bank[2][:].rearrange("p (k n) -> p k n", k=KD), ACT.Copy).then_inc(m_done, 1)

            def copy_bias(b):
                wait(act, cb_mm, held(act, b + 1))
                A(cb_all[:, at(b * KEYS, KEYS)], bank[1][:, 0:KEYS], ACT.Copy).then_inc(cb_done, 1)

            def split_hi(c, f, b):
                wait(act, w_loaded[f], held(act, 48 * b + 48))
                wait(act, w_slot_free, held(act, c + 1))
                A(w_hi[:, f % RING, :], w_raw[:, f, 0:2 * D], ACT.Copy).then_inc(w_hi_done, 1)

            def split_xn2T(s, k):
                if k == 0:
                    wait(act, xn2T_loaded, held(act, 16 * NB * (s + 1)))
                par = parity(act, s)
                A(xn2T_hi[:, par, k, :].rearrange("p o (t n) -> p (o t) n", n=B32), xn2T_raw[:, :, k, :], ACT.Copy).then_inc(xhi_done, 1)

            def hidden(c, f):
                n = held(act, c + 1)
                wait(act, h_mm, n)
                A(h_hi[:, f % 2, :], h_bank[f % 2][:], ACT.Relu, bias=b1_cur[:, f:f + 1], scale=-1.0).then_inc(h_hi_done, 1)
                A(h_full[:, f % 2, :], h_bank[f % 2][:], ACT.Relu, bias=b1_cur[:, f:f + 1], scale=-1.0).then_inc(h_bank_free, 1)

            def ffn_block(s, att=True, last=False, closing=False):
                b = sequence_of(act, s)
                b_next = None if last else sequence_of(act, s + 1)
                for f in range(FC):
                    c = FC * s + f
                    if att and f % 4 == 0:
                        parts = slot_parts(s + LEAD, f // 4, BESIDE)
                    hidden(c, f)
                    if att and f % 4 < 3:
                        parts[f % 4]()
                    if closing and f == 1:
                        ln_v_of(TILES + 2)
                        inverse_roots(TILES + 2)
                    if f + AHEAD < FC:
                        split_hi(c + AHEAD, f + AHEAD, b)
                    elif not last:
                        split_hi(c + AHEAD, f + AHEAD - FC, b_next)
                    if not last and f >= 8 and f % 2 == 0:
                        split_xn2T(s + 1, (f - 8) // 2)

            copy_ctxT(0)
            act.wait_ge(bk_in, 16)
            add_bk(0)
            for h in (0, 2):
                act.wait_ge(wqT_mm, h + 1)
                A(wqT[:, h, :], bank[3 + h][:], ACT.Copy).then_inc(wqT_act, 1)
            act.wait_ge(small_in, 16 * 3)
            A(gates[:], gates[:], ACT.Tanh).then_inc(gates_done, 1)
            nc.scalar.preload_act_table_set("natural_log_exp_and_others")
            act.wait_ge(consts_done, 3)
            ln_v_of(1)
            inverse_roots(1)
            copy_folded(0)
            copy_bias(0)

            def attention_block(m, keys=False, next_ctx_at=None, folded_at=None, last=False):
                for q in range(TPB):
                    part0, part1, part2 = slot_parts(m, q, ALONE)
                    part0()
                    if keys and q == 0:
                        add_bk(m)
                    if q == next_ctx_at:
                        copy_ctxT(m + 1)
                    if q == folded_at:
                        copy_folded(m - 1 if last else m)
                        copy_bias(m - 1 if last else m)
                    if last and q in (1, 2):
                        split_xn2T(0, 2 * q - 2)
                        split_xn2T(0, 2 * q - 1)
                    if last and q == 3:
                        split_hi(0, 0, 0)
                        split_hi(1, 1, 0)
                    part1()
                    part2()

            attention_block(0, next_ctx_at=1)
            with loop(act, 1, BATCH - 1) as m:
                attention_block(m, keys=True, next_ctx_at=2, folded_at=2)
            attention_block(BATCH - 1, keys=True)
            attention_block(LEAD - 1, folded_at=0, last=True)
            copy_xnT(LEAD * TPB + 1, ALONE, xnT_ready, 16)
            split_hi(2, 2, 0)

            with loop(act, 0, BLOCKS - LEAD) as s:
                ffn_block(s)
            ffn_block(BLOCKS - LEAD, att=False, closing=True)
            with loop(act, BLOCKS - LEAD + 1, BLOCKS - 1) as s:
                ffn_block(s, att=False)
            ffn_block(BLOCKS - 1, att=False, last=True)

        @block.vector
        def _(dve):
            V = nc.vector

            def ln_stats(n, w, src):
                V.bn_stats(stats[w][:], src).then_inc(st_done[w], 1)

            def ln_aggregate(w, last):
                agg = V.bn_aggr(mean_var[:, w, :], stats[w][:])
                if last:
                    agg.then_inc(mv_done, 1)

            def ln_rstd(r):
                wait(dve, ysq_done, r)
                V.scalar_tensor_tensor(out=newton[:], in0=mean_var[:, :, 1], scalar=EPS, in1=y_sq[:],
                                       op0=ALU.add, op1=ALU.mult).then_inc(newton_done, 1)
                wait(dve, newton_done, r)
                V.scalar_tensor_tensor(out=neg_rstd[:], in0=newton[:], scalar=S_NEWTON, in1=y_k[:],
                                       op0=ALU.subtract, op1=ALU.mult).then_inc(rstd_done, 1)
                wait(dve, rstd_done, r)

            def ln_apply(w, src, dst, done):
                V.tensor_scalar(dst, src, mean_var[:, w, 0:1], neg_rstd[:, w:w + 1], ALU.subtract, ALU.mult).then_inc(done, 1)

            def output(n, q, bk):
                wait(dve, coef_done, n)
                wait(dve, o_mm, n)
                V.scalar_tensor_tensor(out=x_ring[:, q, :], in0=bk["o"][:], scalar=coef[:], in1=x_ring[:, q, :],
                                       op0=ALU.mult, op1=ALU.add).then_inc(x2_done, 1)
                wait(dve, x2_done, n)
                ln_stats(n, 1, x_ring[:, q, :])

            def slot_parts(m, q, bk, last_tile=False):
                first = type(m) is int and m == 0 and q == 0
                n = held(dve, 4 * m + q + 1)
                b = sequence_of(dve, m)
                keys = at(b * KEYS, KEYS)
                next_q, prev_q = (q + 1) % 4, (q + 3) % 4

                def part0():
                    if not last_tile:
                        wait(dve, x_loaded[next_q], held(dve, 16 * (m + 1) if q < 3 else 16 * (m + 2)))
                        ln_stats(held(dve, n + 1), 0, x_ring[:, next_q, :])
                    if bk is BESIDE and q == 2:
                        block_sum(m)
                        score_terms(m)
                    if not first:
                        output(held(dve, n - 1), prev_q, bk)
                    if bk is ALONE and q == 2 and type(m) is int and m == LEAD - 1:
                        choose_expert(m, bk)

                def part1():
                    if not first:
                        wait(dve, st_done[1], held(dve, n - 1))
                    if not last_tile:
                        wait(dve, st_done[0], held(dve, n + 1))
                    if q == 0:
                        wait(dve, cb_done, held(dve, b + 1))
                    wait(dve, p_done, held(dve, n - 1))
                    wait(dve, s_mm, n)
                    V.tensor_tensor(neg_s[:], bk["s"][:, 0:KEYS], cb_all[:, keys], ALU.subtract).then_inc(negs_done, 1)
                    if not first:
                        ln_aggregate(1, last_tile)
                    if not last_tile:
                        ln_aggregate(0, True)
                    wait(dve, negs_done, n)
                    V.tensor_reduce(neg_max[:], neg_s[:], AX_X, ALU.min).then_inc(s_read, 1)
                    if bk is ALONE and q > 1:
                        transpose_xn2(held(dve, n - 2), q - 2, m)
                    elif bk is ALONE and not (type(m) is int and m == 0):
                        transpose_xn2(held(dve, n - 2), q + 2, m - 1)

                def normed_x2():
                    if not first:
                        wait(dve, xn2T_done, held(dve, n - 2))
                        ln_apply(1, x_ring[:, prev_q, :], xn2[:], xn2_done)

                def part2():
                    ln_rstd(held(dve, n + 1))
                    if bk is BESIDE:
                        normed_x2()
                    if not last_tile:
                        if bk is ALONE:
                            wait(dve, xnT_mm, n)
                        else:
                            wait(dve, xnT_st_done, held(dve, n - LEAD * TPB))
                        ln_apply(0, x_ring[:, next_q, :], xn[:], xn_done)
                    if bk is ALONE:
                        normed_x2()
                    wait(dve, p_done, n)
                    V.reciprocal(p_inv[:], p_sum[:]).then_inc(pinv_done, 1)
                    wait(dve, pinv_done, n)
                    V.tensor_scalar(coef[:], p_inv[:], gate_x[:], NORM, ALU.mult, ALU.mult).then_inc(coef_done, 1)
                    if bk is BESIDE and q == 2:
                        choose_expert(m, bk)
                    if bk is ALONE and q == 1 and not (type(m) is int and m == 0):
                        block_sum(m)
                    if bk is ALONE and q == 1 and type(m) is int and m == LEAD - 1:
                        score_terms(m)

                def part3():
                    if bk is BESIDE:
                        if q > 0:
                            transpose_xn2(held(dve, n - 1), q - 1, m)
                        else:
                            transpose_xn2(held(dve, n - 1), 3, m - 1)
                    if not last_tile and bk is BESIDE:
                        turn_xn(n + 1, n - (LEAD * TPB - 1))
                return part0, part1, part2, part3

            def add_bv(b):
                wait(dve, v_mm, held(dve, b + 1))
                V.tensor_tensor(v_all[:, at(b, 1), :].rearrange("p o n -> p (o n)"), bank[0][:], bv_sb, ALU.add).then_inc(v_done, 1)

            def attention_block(m, bv_after=None):
                for q in range(TPB):
                    part0, part1, part2, _ = slot_parts(m, q, ALONE)
                    part0()
                    part1()
                    part2()
                    if q == bv_after:
                        add_bv(m)

            def turn_xn(n, turn):
                wait(dve, xnT_stored, held(dve, 16 * NB * (turn - 1)))
                wait(dve, xn_done, n if type(n) is int else held(dve, n))
                V.transpose(xnT_st[:].bitcast(U32), xn[:].rearrange("p (k a c) -> p a k c", k=KD, a=NB).bitcast(U32)).then_inc(xnT_st_done, 1)

            def transpose_xn2(n, q, m):
                wait(dve, xn2T_stored[q % 2], held(dve, 32 * m + 16 * (q // 2)))
                wait(dve, tiles_summed, held(dve, 3 * m + (-1, 0, 1, 1)[q]))
                wait(dve, xn2_done, n)
                V.transpose(xn2T_st[:, q % 2].bitcast(U32), xn2[:].rearrange("p (k a c) -> p a k c", k=KD, a=NB).bitcast(U32)).then_inc(xn2T_done, 1)

            def block_sum(m):
                in_seq = (m - 1) % BPS if type(m) is int else nc.s_assert_within(dve.snap((m + (BPS - 1)) & (BPS - 1)), 0, BPS - 1, skip_runtime_bounds_check_because="the loop ends at a fixed block")
                wait(dve, tiles_summed, held(dve, 3 * m))
                V.reduce_sum(blk_sums[:, :, :, at(in_seq, 1)].rearrange("p a k o -> p (a k) o"),
                             tile_sum[:].rearrange("p (g c) -> p g c", c=B32), AX_X).then_inc(blk_done, 1)

            def score_terms(m):
                mv = held(dve, m - (BPS - 1))
                wait(dve, blk_done, held(dve, m))
                V.reduce_sum(seq_sums[:].rearrange("p a k -> p (a k)"), blk_sums[:].rearrange("p a k b -> p (a k) b"), AX_X).then_inc(seq_done, 1)
                wait(dve, seq_done, mv)
                V.tensor_tensor(weighted[:].rearrange("p e (a k) -> p e a k", a=NB), wr_sb[:].rearrange("p k a e -> p e a k"),
                                seq_sums[:].rearrange("p (o a) k -> p o a k", o=1).to_broadcast([P, EXPERTS, NB, KD]),
                                ALU.mult).then_inc(weighted_done, 1)
                wait(dve, weighted_done, mv)
                V.reduce_sum(score_parts[:], weighted[:], AX_X).then_inc(parts_done, 1)

            def choose_expert(m, bk):
                mv = held(dve, m - (BPS - 1))
                wait(dve, router_mm, mv)
                V.scalar_tensor_tensor(out=logits[:], in0=bk["router"][0:1, 0:EXPERTS], scalar=-1.0 / SEQ, in1=br_sb[:],
                                       op0=ALU.mult, op1=ALU.add).then_inc(logits_done, 1)
                wait(dve, logits_done, mv)
                V.reduce_max(top[:], logits[:], AX_X).then_inc(top_done, 1)
                wait(dve, top_done, mv)
                V.scalar_tensor_tensor(out=reach[:], in0=logits[:], scalar=top[:], in1=rank_down[:],
                                       op0=ALU.is_ge, op1=ALU.mult).then_inc(reach_done, 1)
                wait(dve, reach_done, mv)
                V.reduce_max(best_rank[:], reach[:], AX_X).then_inc(rank_done, 1)
                wait(dve, rank_done, mv)
                V.tensor_scalar(expert[:, at(m, 1)], best_rank[:], -1.0, float(EXPERTS), ALU.mult, ALU.add).then_inc(expert_done, 1)

            def hidden_lo(c, f):
                wait(dve, h_bank_free, held(dve, c + 3))
                V.tensor_tensor(h_lo[:, f % 2, :], h_full[:, f % 2, :], h_hi[:, f % 2, :].bitcast(F32),
                                ALU.subtract).then_inc(h_lo_done, 1)

            def split_xn2T(s, k):
                wait(dve, xhi_done, held(dve, KD * s + k + 1))
                par = parity(dve, s)
                V.tensor_tensor(xn2T_lo[:, par, k, :].rearrange("p o (t n) -> p (o t) n", n=B32), xn2T_raw[:, :, k, :],
                                xn2T_hi[:, par, k, :].rearrange("p o (t n) -> p (o t) n", n=B32).bitcast(F32),
                                ALU.subtract).then_inc(xlo_done, 1)

            def add_b2(s, t):
                if t == 0:
                    wait(dve, x2_loaded, held(dve, 16 * s + 16))
                    wait(dve, b2_loaded, held(dve, 16 * (s // BPS + 1) if type(s) is int else 16 * ((s >> 2) + 1)))
                V.scalar_tensor_tensor(out=x2_blk[:, t, :], in0=b2_cur[:], scalar=gate_f[:], in1=x2_blk[:, t, :],
                                       op0=ALU.mult, op1=ALU.add).then_inc(b2_added, 1)

            def finish(s, t):
                if t < TPB - 1:
                    wait(dve, out_mm, held(dve, (TPB - 1) * s + t + 1))
                else:
                    wait(dve, w_slot_free, held(dve, RING + FC * s + FC))
                V.scalar_tensor_tensor(out=x2_blk[:, t, :], in0=out_bank[t][:], scalar=gate_f[:], in1=x2_blk[:, t, :],
                                       op0=ALU.mult, op1=ALU.add).then_inc(out_bank_free, 1)

            def ffn_block(s, att=True, last_att=False, last=False, closing=False):
                for f in range(FC):
                    c = FC * s + f
                    if att and f % 4 == 0:
                        parts = slot_parts(s + LEAD, f // 4, BESIDE, last_att and f == 12)
                    hidden_lo(c, f)
                    if att:
                        parts[f % 4]()
                    if closing and f == 0:
                        output(TILES, 3, BESIDE)
                    if closing and f == 1:
                        wait(dve, st_done[1], TILES)
                        ln_aggregate(1, True)
                    if closing and f == 3:
                        wait(dve, xn2T_done, TILES - 1)
                        ln_rstd(TILES + 2)
                        ln_apply(1, x_ring[:, 3, :], xn2[:], xn2_done)
                        transpose_xn2(TILES, 3, BLOCKS - 1)
                    if closing and f == 8:
                        block_sum(BLOCKS)
                        score_terms(BLOCKS)
                    if closing and f == 9:
                        choose_expert(BLOCKS, BESIDE)
                    if not last and f >= 8 and f % 2 == 0:
                        split_xn2T(s + 1, (f - 8) // 2)
                    if f >= 8 and f % 2 == 1:
                        add_b2(s, (f - 9) // 2)
                wait(dve, b2_added, held(dve, TPB * s + TPB))
                for t in range(TPB):
                    finish(s, t)

            V.memset(probs[:], 0.0).then_inc(warm_done, 1)
            V.memset(eps_c[:], EPS).then_inc(consts_done, 1)
            V.memset(lnk_c[:], LN_K).then_inc(consts_done, 1)
            V.memset(blk_sums[:], 0.0)
            V.memset(ones[:], 1.0)
            V.memset(mean_var[:], 1.0).then_inc(consts_done, 1)
            dve.wait_ge(consts_done, 3)
            dve.wait_ge(x_loaded[0], 16)
            ln_stats(1, 0, x_ring[:, 0, :])
            dve.wait_ge(st_done[0], 1)
            ln_aggregate(0, True)
            for h in (1, 3):
                dve.wait_ge(wqT_mm, h + 1)
                V.tensor_copy(wqT[:, h, :], bank[3 + h][:]).then_inc(wqT_dve, 1)
            dve.wait_ge(bq_in, 16)
            V.tensor_copy(bqb, bq_sb[:].rearrange("p (k o) -> p k o", o=1).to_broadcast([P, KD, P])).then_inc(consts_done, 1)
            ln_rstd(1)
            ln_apply(0, x_ring[:, 0, :], xn[:], xn_done)
            dve.wait_ge(gates_done, 1)
            V.tensor_copy(gate_x[:], gates[:, 0:1])
            V.tensor_copy(gate_f[:], gates[:, 1:2]).then_inc(consts_done, 1)
            dve.wait_ge(router_in, 16 * (NB + 2))
            dve.wait_ge(consts_done, 5)

            attention_block(0, bv_after=0)
            with loop(dve, 1, BATCH - 1) as m:
                attention_block(m, bv_after=0)
            attention_block(BATCH - 1, bv_after=0)
            attention_block(LEAD - 1)

            transpose_xn2(LEAD * TPB - 1, 2, LEAD - 1)
            dve.wait_ge(xnT_mm, LEAD * TPB + 1)
            dve.sem_inc(xnT_st_done, 1)

            with loop(dve, 0, BLOCKS - LEAD - 1) as s:
                ffn_block(s)
            ffn_block(BLOCKS - LEAD - 1, last_att=True)
            ffn_block(BLOCKS - LEAD, att=False, closing=True)
            with loop(dve, BLOCKS - LEAD + 1, BLOCKS - 1) as s:
                ffn_block(s, att=False)
            ffn_block(BLOCKS - 1, att=False, last=True)

        @block.gpsimd
        def _(pool):
            def add_tile(m, q):
                total, stage = tile_sum[:], xn2T_st[:].rearrange("p o a k c -> p o (a k c)")
                if q == 1 and not (type(m) is int and m == 0):
                    wait(pool, blk_done, held(pool, m))
                if q > 1:
                    wait(pool, tiles_summed, held(pool, 3 * m + q - 1))
                wait(pool, xn2T_done, held(pool, 4 * m + q + 1))
                nc.gpsimd.tensor_tensor(total, stage[:, 0] if q == 1 else total, stage[:, q % 2], ALU.add).then_inc(tiles_summed, 1)

            for q in range(1, TPB):
                add_tile(0, q)
            with loop(pool, 1, LEAD - 1) as m:
                for q in range(1, TPB):
                    add_tile(m, q)
            for k in range(KD):
                pool.wait_ge(xhi_done, k + 1)
                nc.gpsimd.tensor_tensor(xn2T_lo[:, 0, k, :].rearrange("p (t n) -> p t n", n=B32), xn2T_raw[:, :, k, :],
                                        xn2T_hi[:, 0, k, :].rearrange("p (t n) -> p t n", n=B32).bitcast(F32),
                                        ALU.subtract).then_inc(xlo_done, 1)
            def ffn_block(s, end_before=True, begin=True, begin_before=False):
                for f in range(FC):
                    wait(pool, w_hi_done, held(pool, FC * s + f + 1))
                    nc.gpsimd.tensor_tensor(w_lo[:, f % RING, :], w_raw[:, f, 0:2 * D],
                                            w_hi[:, f % RING, :].bitcast(F32), ALU.subtract)
                    nc.gpsimd.tensor_copy(b1_cur[:, f:f + 1], w_raw[:, f, 2 * D:2 * D + 1]).then_inc(w_lo_done, 1)
                    if begin_before and f == 0:
                        add_tile(s + LEAD - 1, 1)
                    if end_before and f in (2, 5):
                        add_tile(s + LEAD - 1, 2 if f == 2 else 3)
                    if begin and f == 14:
                        add_tile(s + LEAD, 1)

            ffn_block(0, begin_before=True)
            with loop(pool, 1, BLOCKS - LEAD) as s:
                ffn_block(s)
            ffn_block(BLOCKS - LEAD, begin=False)
            with loop(pool, BLOCKS - LEAD + 1, BLOCKS) as s:
                ffn_block(s, end_before=False, begin=False)


_INS = ["x", "ctx_1024", "g_xattn", "g_ffn", "L0_xattn_Wq", "L0_xattn_bq", "L0_xattn_Wk", "L0_xattn_bk",
        "L0_xattn_Wv", "L0_xattn_bv", "L0_ffn_Wr", "L0_ffn_br", "L0_ffn_W1", "L0_ffn_b1", "L0_ffn_W2", "L0_ffn_b2"]


def kernel(**inputs):
    import numpy as np
    import concourse.bacc as bacc
    from concourse.bass_utils import run_bass_kernel_spmd

    nc = bacc.Bacc("TRN2", target_bir_lowering=False, num_devices=1)
    arrays, args = {}, []
    for name in _INS:
        a = np.ascontiguousarray(inputs[name])
        if name == "x":
            a = a.reshape(BLOCKS, TPB, P, D)
        arrays[f"in_{name}"] = a
        args.append(nc.dram_tensor(f"in_{name}", a.shape, mybir.dt.from_np(a.dtype), kind="ExternalInput").ap())
    arrays["identity"] = np.eye(P, dtype=np.float32)
    args.append(nc.dram_tensor("identity", (P, P), F32, kind="ExternalInput").ap())
    arrays["rank_down"] = np.arange(EXPERTS, 0, -1, dtype=np.float32)[None, :]
    args.append(nc.dram_tensor("rank_down", (1, EXPERTS), F32, kind="ExternalInput").ap())
    out = nc.dram_tensor("out", (BLOCKS, TPB, P, D), F32, kind="ExternalOutput").ap()
    gated_block(nc, *args, out.rearrange("s t p n -> s p t n"))
    got = run_bass_kernel_spmd(nc, [arrays], core_ids=[0])
    return got.results[0]["out"].reshape(BATCH, SEQ, D)
```
